# Optimizing a Trainium2 kernel written in Bass

```python
import numpy as np
import jax
import jax.numpy as jnp

def _softmax(x, axis=-1):
    return jax.nn.softmax(x, axis=axis)

def _gelu(x):
    return jax.nn.gelu(x, approximate=True)

def _silu(x):
    return jax.nn.silu(x)

def _sigmoid(x):
    return jax.nn.sigmoid(x)

def _layernorm(x, axis=-1, eps=1e-05):
    m = jnp.mean(x, axis=axis, keepdims=True)
    v = jnp.var(x, axis=axis, keepdims=True)
    return (x - m) / jnp.sqrt(v + eps)

def _scatter_add(tgt, idx, src, axis=0):
    return tgt.at[idx].add(src)

def _segment_sum(src, seg, n):
    return jax.ops.segment_sum(src, seg, n)
kernel_name = 'mk_adaln_d2_jaxref_r8_0394e6'

def setup_inputs(seed: int=0):
    np.random.seed(seed)
    _w = jnp.asarray

    def _L0_attn_setup():
        import jax, jax.numpy as jnp
        import numpy as np
        EPS = 1e-05
        NUM_HEADS = 16

        def _yat_dense(x, w, b, alpha):
            dot = x @ w
            dist = jnp.sum(x * x, axis=-1, keepdims=True) + jnp.sum(w * w, axis=0) - 2.0 * dot
            y = dot * dot / (dist + EPS) + b
            dout = w.shape[1]
            scale = (jnp.sqrt(jnp.float32(dout)) / jnp.log(jnp.float32(1 + dout))) ** alpha
            return y * scale
        key = jax.random.key(seed)
        ks = jax.random.split(key, 5)
        B, S, D = (4, 128, 128)
        sc = jnp.float32(1.0 / np.sqrt(D))
        f32 = jnp.float32
        return {'inputs_q': jax.random.normal(ks[0], (B, S, D), f32), 'wq': jax.random.normal(ks[1], (D, D), f32) * sc, 'bq': jnp.zeros((D,), f32), 'aq': jnp.ones((1,), f32), 'wk': jax.random.normal(ks[2], (D, D), f32) * sc, 'bk': jnp.zeros((D,), f32), 'ak': jnp.ones((1,), f32), 'wv': jax.random.normal(ks[3], (D, D), f32) * sc, 'bv': jnp.zeros((D,), f32), 'av': jnp.ones((1,), f32), 'wo': jax.random.normal(ks[4], (D, D), f32) * sc, 'bo': jnp.zeros((D,), f32)}
    _L0_attn_in = _L0_attn_setup()

    def _L0_ffn_setup():
        import jax, jax.numpy as jnp
        import numpy as np
        TEMPERATURE = 0.5
        CAPACITY_FACTOR = 1.25
        TOP_K = 1
        key = jax.random.key(seed)
        ks = jax.random.split(key, 5)
        B, S, D, H, E = (4, 256, 128, 256, 8)
        s = 0.02
        return {'x': jax.random.normal(ks[0], (B, S, D), jnp.float32), 'gate_w': jax.random.normal(ks[1], (E, D), jnp.float32) * s, 'gate_b': jnp.zeros((E,), jnp.float32), 'rms_w': jnp.ones((E,), jnp.float32), 'w1': jax.random.normal(ks[2], (E, D, H), jnp.float32) * s, 'b1': jnp.zeros((E, H), jnp.float32), 'w2': jax.random.normal(ks[3], (E, H, D), jnp.float32) * s, 'b2': jnp.zeros((E, D), jnp.float32)}
    _L0_ffn_in = _L0_ffn_setup()
    _L0_c = _w((lambda *s: np.random.randn(*s).astype(np.float32) * 0.05)(8, 128))
    _L0_wmod = _w((lambda *s: np.random.randn(*s).astype(np.float32) * 0.05)(128, 6 * 128) * 128 ** (-0.5))

    def _L1_attn_setup():
        import jax, jax.numpy as jnp
        import numpy as np
        import math
        B, S, D = (4, 256, 128)
        H = 16
        HD = D // H
        DL = 32
        LAMBDA_DECAY = 0.01
        key = jax.random.key(seed)
        ks = jax.random.split(key, 8)
        sc = lambda fan_in: 1.0 / math.sqrt(fan_in)
        return {'x': jax.random.normal(ks[0], (B, S, D), dtype=jnp.float32), 'W_q': jax.random.normal(ks[1], (D, D), dtype=jnp.float32) * sc(D), 'W_k': jax.random.normal(ks[2], (D, D), dtype=jnp.float32) * sc(D), 'W_v': jax.random.normal(ks[3], (D, D), dtype=jnp.float32) * sc(D), 'W_o': jax.random.normal(ks[4], (D, D), dtype=jnp.float32) * sc(D), 'W_down_kv': jax.random.normal(ks[5], (D, DL), dtype=jnp.float32) * sc(D), 'W_up_k': jax.random.normal(ks[6], (DL, D), dtype=jnp.float32) * sc(DL), 'W_up_v': jax.random.normal(ks[7], (DL, D), dtype=jnp.float32) * sc(DL)}
    _L1_attn_in = _L1_attn_setup()

    def _L1_ffn_setup():
        import jax, jax.numpy as jnp
        import numpy as np
        LORA_DIM = 16
        LORA_TOKEN_INDEX = 1
        B, S, D, H = (4, 256, 128, 512)
        key = jax.random.key(seed)
        ks = jax.random.split(key, 6)
        x = jax.random.normal(ks[0], (B, S, D), dtype=jnp.float32)
        W1 = jax.random.normal(ks[1], (H, D), dtype=jnp.float32) * 0.02
        b1 = jnp.zeros((H,), dtype=jnp.float32)
        W2 = jax.random.normal(ks[2], (D, H), dtype=jnp.float32) * 0.02
        b2 = jnp.zeros((D,), dtype=jnp.float32)
        scale = jnp.asarray(0.001, dtype=jnp.float32)
        return {'x': x, 'W1': W1, 'b1': b1, 'W2': W2, 'b2': b2, 'scale': scale}
    _L1_ffn_in = _L1_ffn_setup()
    _L1_c = _w((lambda *s: np.random.randn(*s).astype(np.float32) * 0.05)(8, 128))
    _L1_wmod = _w((lambda *s: np.random.randn(*s).astype(np.float32) * 0.05)(128, 6 * 128) * 128 ** (-0.5))
    _d = {'L0_attn_inputs_q': _L0_attn_in['inputs_q'], 'L0_attn_wq': _L0_attn_in['wq'], 'L0_attn_bq': _L0_attn_in['bq'], 'L0_attn_aq': _L0_attn_in['aq'], 'L0_attn_wk': _L0_attn_in['wk'], 'L0_attn_bk': _L0_attn_in['bk'], 'L0_attn_ak': _L0_attn_in['ak'], 'L0_attn_wv': _L0_attn_in['wv'], 'L0_attn_bv': _L0_attn_in['bv'], 'L0_attn_av': _L0_attn_in['av'], 'L0_attn_wo': _L0_attn_in['wo'], 'L0_attn_bo': _L0_attn_in['bo'], 'L0_ffn_gate_w': _L0_ffn_in['gate_w'], 'L0_ffn_gate_b': _L0_ffn_in['gate_b'], 'L0_ffn_rms_w': _L0_ffn_in['rms_w'], 'L0_ffn_w1': _L0_ffn_in['w1'], 'L0_ffn_b1': _L0_ffn_in['b1'], 'L0_ffn_w2': _L0_ffn_in['w2'], 'L0_ffn_b2': _L0_ffn_in['b2'], 'L0_c': _L0_c, 'L0_wmod': _L0_wmod, 'L1_attn_W_q': _L1_attn_in['W_q'], 'L1_attn_W_k': _L1_attn_in['W_k'], 'L1_attn_W_v': _L1_attn_in['W_v'], 'L1_attn_W_o': _L1_attn_in['W_o'], 'L1_attn_W_down_kv': _L1_attn_in['W_down_kv'], 'L1_attn_W_up_k': _L1_attn_in['W_up_k'], 'L1_attn_W_up_v': _L1_attn_in['W_up_v'], 'L1_ffn_W1': _L1_ffn_in['W1'], 'L1_ffn_b1': _L1_ffn_in['b1'], 'L1_ffn_W2': _L1_ffn_in['W2'], 'L1_ffn_b2': _L1_ffn_in['b2'], 'L1_ffn_scale': _L1_ffn_in['scale'], 'L1_c': _L1_c, 'L1_wmod': _L1_wmod}
    _x0 = _d['L0_attn_inputs_q']
    _d['L0_attn_inputs_q'] = jax.random.normal(jax.random.fold_in(jax.random.key(seed), 1), (8, 512, 128), dtype=_x0.dtype)
    del _x0
    return _d

def reference(L0_attn_inputs_q, L0_attn_wq, L0_attn_bq, L0_attn_aq, L0_attn_wk, L0_attn_bk, L0_attn_ak, L0_attn_wv, L0_attn_bv, L0_attn_av, L0_attn_wo, L0_attn_bo, L0_ffn_gate_w, L0_ffn_gate_b, L0_ffn_rms_w, L0_ffn_w1, L0_ffn_b1, L0_ffn_w2, L0_ffn_b2, L0_c, L0_wmod, L1_attn_W_q, L1_attn_W_k, L1_attn_W_v, L1_attn_W_o, L1_attn_W_down_kv, L1_attn_W_up_k, L1_attn_W_up_v, L1_ffn_W1, L1_ffn_b1, L1_ffn_W2, L1_ffn_b2, L1_ffn_scale, L1_c, L1_wmod):

    def _L0_attn_ref(inputs_q, wq, bq, aq, wk, bk, ak, wv, bv, av, wo, bo):
        import jax, jax.numpy as jnp
        import numpy as np
        EPS = 1e-05
        NUM_HEADS = 16

        def _yat_dense(x, w, b, alpha):
            dot = x @ w
            dist = jnp.sum(x * x, axis=-1, keepdims=True) + jnp.sum(w * w, axis=0) - 2.0 * dot
            y = dot * dot / (dist + EPS) + b
            dout = w.shape[1]
            scale = (jnp.sqrt(jnp.float32(dout)) / jnp.log(jnp.float32(1 + dout))) ** alpha
            return y * scale
        B, S, D = inputs_q.shape
        H = NUM_HEADS
        Dh = D // H
        q = _yat_dense(inputs_q, wq, bq, aq).reshape(B, S, H, Dh)
        k = _yat_dense(inputs_q, wk, bk, ak).reshape(B, S, H, Dh)
        v = _yat_dense(inputs_q, wv, bv, av).reshape(B, S, H, Dh)
        attn = jnp.einsum('bqhd,bkhd->bhqk', q, k)
        sq = attn * attn
        qn = jnp.sum(q * q, axis=-1)
        kn = jnp.sum(k * k, axis=-1)
        nsum = (qn + kn).transpose(0, 2, 1)[..., None]
        w = sq / (nsum - 2.0 * sq + EPS)
        w = jax.nn.softmax(w, axis=-1)
        out = jnp.einsum('bhqk,bkhd->bqhd', w, v).reshape(B, S, D)
        return out @ wo + bo

    def _L0_ffn_ref(x, gate_w, gate_b, rms_w, w1, b1, w2, b2):
        import jax, jax.numpy as jnp
        import numpy as np
        TEMPERATURE = 0.5
        CAPACITY_FACTOR = 1.25
        TOP_K = 1
        B, S, D = x.shape
        E = gate_w.shape[0]
        xf = x.reshape(-1, D)
        N = xf.shape[0]
        logits = xf @ gate_w.T + gate_b
        eps = jnp.finfo(logits.dtype).eps
        ms = jnp.mean(logits * logits, axis=-1, keepdims=True)
        logits = logits * jax.lax.rsqrt(ms + eps) * rms_w
        gates = jax.nn.softmax(logits / TEMPERATURE, axis=-1)
        g, idx = jax.lax.top_k(gates, TOP_K)
        g, idx = (g[:, 0], idx[:, 0])
        capacity = min(int(np.ceil(N * TOP_K / E * CAPACITY_FACTOR)), N)
        counts = jnp.zeros((E,), jnp.int32).at[idx].add(1)
        active = (counts > 0) & (capacity >= 1)
        mask = active[idx].astype(gates.dtype)
        masked = g * mask
        norm_g = masked / (masked + 1e-06)
        h = jax.nn.gelu(jnp.einsum('nd,edh->neh', xf, w1) + b1, approximate=False)
        y = jnp.einsum('neh,ehd->ned', h, w2) + b2
        out = (y * norm_g[:, None, None]).sum(axis=1)
        return out.reshape(B, S, D)

    def _L1_attn_ref(x, W_q, W_k, W_v, W_o, W_down_kv, W_up_k, W_up_v):
        import jax, jax.numpy as jnp
        import numpy as np
        import math
        B, S, D = (4, 256, 128)
        H = 16
        HD = D // H
        DL = 32
        LAMBDA_DECAY = 0.01
        b, s, d = x.shape
        q = x @ W_q
        k = x @ W_k
        v = x @ W_v
        latent_kv = (k + v) @ W_down_kv
        k_rec = (latent_kv @ W_up_k).reshape(b, s, H, HD).transpose(0, 2, 1, 3)
        v_rec = (latent_kv @ W_up_v).reshape(b, s, H, HD).transpose(0, 2, 1, 3)
        qh = q.reshape(b, s, H, HD).transpose(0, 2, 1, 3)
        scores = jnp.einsum('bhqd,bhkd->bhqk', qh, k_rec) / math.sqrt(d)
        t = jnp.arange(s, dtype=jnp.float32)
        decay = jnp.exp(-LAMBDA_DECAY * jnp.abs(t[:, None] - t[None, :]))
        scores = scores * decay[None, None, :, :]
        attn = jax.nn.softmax(scores, axis=-1)
        out = jnp.einsum('bhqk,bhkd->bhqd', attn, v_rec)
        out = out.transpose(0, 2, 1, 3).reshape(b, s, d)
        return out @ W_o

    def _L1_ffn_ref(x, W1, b1, W2, b2, scale):
        import jax, jax.numpy as jnp
        import numpy as np
        LORA_DIM = 16
        LORA_TOKEN_INDEX = 1
        B, S, D, H = (4, 256, 128, 512)
        Bx, Sx, Dx = x.shape
        Hx = W1.shape[0]
        lt = jax.lax.dynamic_slice_in_dim(x, LORA_TOKEN_INDEX, LORA_DIM, axis=1)
        even = lt[:, ::2, :]
        odd = lt[:, 1::2, :]
        m1 = (even[:, :4, :, None] * odd[:, :4, None, :]).reshape(Bx, Hx, Dx)
        m2 = (even[:, 4:, :, None] * odd[:, 4:, None, :]).reshape(Bx, Dx, Hx)
        h = jnp.einsum('bsd,hd->bsh', x, W1) + scale * jnp.einsum('bsd,bhd->bsh', x, m1) + b1
        h = jax.nn.gelu(h, approximate=False)
        out = jnp.einsum('bsh,oh->bso', h, W2) + scale * jnp.einsum('bsh,boh->bso', h, m2) + b2
        return out
    x = L0_attn_inputs_q
    mod = (_silu(L0_c) @ L0_wmod).reshape(L0_c.shape[0], 6, 1, -1)
    sa, ca, ga, sb, cb, gb = (mod[:, 0], mod[:, 1], mod[:, 2], mod[:, 3], mod[:, 4], mod[:, 5])
    ga = (2 * (ga >= 0) - 1) * jnp.maximum(jnp.abs(ga), 0.25)
    gb = (2 * (gb >= 0) - 1) * jnp.maximum(jnp.abs(gb), 0.25)
    h = _layernorm(x, axis=-1) * (1 + ca) + sa
    x = x + ga * _L0_attn_ref(h, L0_attn_wq, L0_attn_bq, L0_attn_aq, L0_attn_wk, L0_attn_bk, L0_attn_ak, L0_attn_wv, L0_attn_bv, L0_attn_av, L0_attn_wo, L0_attn_bo)
    h = _layernorm(x, axis=-1) * (1 + cb) + sb
    x = x + gb * _L0_ffn_ref(h, L0_ffn_gate_w, L0_ffn_gate_b, L0_ffn_rms_w, L0_ffn_w1, L0_ffn_b1, L0_ffn_w2, L0_ffn_b2)
    mod = (_silu(L1_c) @ L1_wmod).reshape(L1_c.shape[0], 6, 1, -1)
    sa, ca, ga, sb, cb, gb = (mod[:, 0], mod[:, 1], mod[:, 2], mod[:, 3], mod[:, 4], mod[:, 5])
    ga = (2 * (ga >= 0) - 1) * jnp.maximum(jnp.abs(ga), 0.25)
    gb = (2 * (gb >= 0) - 1) * jnp.maximum(jnp.abs(gb), 0.25)
    h = _layernorm(x, axis=-1) * (1 + ca) + sa
    x = x + ga * _L1_attn_ref(h, L1_attn_W_q, L1_attn_W_k, L1_attn_W_v, L1_attn_W_o, L1_attn_W_down_kv, L1_attn_W_up_k, L1_attn_W_up_v)
    h = _layernorm(x, axis=-1) * (1 + cb) + sb
    x = x + gb * _L1_ffn_ref(h, L1_ffn_W1, L1_ffn_b1, L1_ffn_W2, L1_ffn_b2, L1_ffn_scale)
    return x

_drawn_inputs = setup_inputs


def setup_inputs(seed=0):
    import zlib

    import numpy as np

    out = dict(_drawn_inputs(seed))
    spreads = {'L0_attn_bq': (0.0, 0.8),
     'L0_attn_bk': (0.0, 0.8),
     'L0_attn_bv': (0.0, 0.1),
     'L0_attn_bo': (0.0, 0.3),
     'L0_ffn_gate_b': (0.0, 0.8),
     'L0_ffn_rms_w': (1.0, 0.6),
     'L0_ffn_b1': (0.0, 0.697),
     'L0_ffn_b2': (0.0, 0.1),
     'L1_ffn_b1': (0.0, 0.8),
     'L1_ffn_b2': (0.0, 0.302)}
    factors = {'L0_attn_wq': 8.0,
     'L0_attn_wk': 8.0,
     'L0_attn_wv': 8.0,
     'L0_ffn_gate_w': 8.0,
     'L1_attn_W_q': 6.06,
     'L1_attn_W_up_k': 6.073,
     'L1_ffn_W1': 4.173,
     'L1_ffn_W2': 3.708}
    for name, (base, spread) in spreads.items():
        noise = np.random.default_rng([zlib.crc32(name.encode()), seed]).standard_normal(out[name].shape)
        drawn = base * np.exp(spread * noise) if base else spread * noise
        out[name] = jnp.asarray(drawn.astype(out[name].dtype))
    for name, factor in factors.items():
        out[name] = (out[name] * factor).astype(out[name].dtype)
    return out
```

```python
import math
from contextlib import ExitStack

import numpy as np
import concourse.bass as bass
from concourse import mybir

F32 = mybir.dt.float32
BF16 = mybir.dt.bfloat16
U32 = mybir.dt.uint32
ALU = mybir.AluOpType
ACT = mybir.ActivationFunctionType
AX_X = mybir.AxisListType.X

B, S, D = 8, 512, 128
H, DH = 16, 8
P = 128
NT = S // P
GH = 4
NG = H // GH
GROUPS = B * NG
HEADS = B * H
SPLITS = 3
KROWS = SPLITS * SPLITS * DH
VC = DH + 1
EX, HID = 8, 256
EU = EX * HID // P
MH = 512
MU = MH // P
LN_EPS = 1e-5
ATT_EPS = 1e-5
RMS_EPS = float(np.finfo(np.float32).eps)
NORM_EPS = 1e-6
YAT_BASE = math.sqrt(D) / math.log(1 + D)
DOT_SCALE = 1 / math.sqrt(D)
ZERO_GUARD = 1e-12
SA, CA, GA, SB, CB, GB = range(6)
LAG = {"B": 3, "D": 2}
UNROLL = 8


class Order:

    def __init__(self, eng, sem, base):
        self.eng, self.sem, self.base, self.n = eng, sem, base, 0

    def __call__(self, ins):
        self.n += 1
        ins.then_inc(self.sem, 1)
        self.eng.wait_ge(self.sem, self.base + self.n)


OWN = {"dveA": 34, "dveC": 38, "dveE": 16, "actA": 2, "actC": 3, "actE": 1}

SCORES0 = 2 * GH * 2 - 7
TURNED0 = 13
PV0 = 2
DOWN0 = 4
STACK = 2 * SPLITS * SPLITS * 16


class At:

    def __init__(self, turn):
        self.turn, self.group, self.head = turn, turn * 2, turn * UNROLL


def build(nc, xT, cT, wmod, wqkv, bqkv, alpha, wo0, bo0, gwT, gb, rms, w1, b1, w2, b2,
          l1w, l1down, l1up, l1wo, mw1, mb1, mw2, mb2, scale, ident_in, blk_in, decay_in,
          parts, out):
    ctx = ExitStack()
    with ctx:
        def sb(name, shape, dt=F32):
            return ctx.enter_context(nc.sbuf_tensor(name, shape, dt))

        sems = {}

        def sem(name):
            if name not in sems:
                sems[name] = ctx.enter_context(nc.semaphore(name))
            return sems[name]

        x = sb("x", [P, B * S])
        vall = sb("vall", [P, GROUPS, NT, GH, VC])
        vg = sb("vg", [P, 2, NT, GH, 32])
        oall = sb("oall", [P, GROUPS, NT, GH * DH])
        qst = sb("qst", [P, 2, GH, S], BF16)
        kst = sb("kst", [P, 2, GH, S], BF16)
        decay = sb("decay", [P, NT, S])
        big = sb("big", [P, 40 * S])
        small = sb("small", [P, 256])
        pq = sb("pq", [P, SPLITS, S], BF16)
        pk = sb("pk", [P, SPLITS, S], BF16)
        mod = sb("mod", [P, B, 12])
        mb = sb("mb", [P, 12])
        ident = sb("ident", [P, P])
        mean_w = sb("mean_w", [P, P])
        ones = sb("ones", [P, P])
        blk = sb("blk", [P, P])
        wmod_sb = sb("wmod_sb", [P, 2, 6 * D])
        c_sb = sb("c_sb", [P, 2, B])
        sil = sb("sil", [P, 4, 2, B])
        w_qkv = sb("w_qkv", [P, 3, D])
        b_qkv = sb("b_qkv", [P, 3])
        al = sb("al", [P, 3])
        s_base = sb("s_base", [P, 3])
        s_yat = sb("s_yat", [P, 3])
        wn = sb("wn", [P, 3])
        wo0_sb = sb("wo0_sb", [P, D])
        bo0_sb = sb("bo0_sb", [P, 1])
        gw_sb = sb("gw_sb", [P, EX])
        gb_sb = sb("gb_sb", [P, EX])
        rms_sb = sb("rms_sb", [P, EX])
        w1_sb = sb("w1_sb", [P, EU, P])
        b1_sb = sb("b1_sb", [P, EU])
        w2_sb = sb("w2_sb", [P, EU, D])
        b2_sb = sb("b2_sb", [P, EX])
        b2s = sb("b2s", [P, 1])
        l1w_sb = sb("l1w_sb", [P, 3, D])
        dn_sb = sb("dn_sb", [P, 32])
        up_sb = sb("up_sb", [32, 2, D])
        wo1_sb = sb("wo1_sb", [P, D])
        mw1_sb = sb("mw1_sb", [P, MH])
        mb1_sb = sb("mb1_sb", [P, MU])
        mw2_sb = sb("mw2_sb", [P, MU, D])
        mb2_sb = sb("mb2_sb", [P, 1])
        sc_sb = sb("sc_sb", [P, 1])
        ps = ctx.enter_context(nc.psum_tensor("ps", [P, 8, 512], F32))

        HS = NT * S
        Y = [big[:, n * HS:(n + 1) * HS] for n in range(4)]
        A = [big[:, (4 + n) * HS:(5 + n) * HS] for n in range(2)]
        PT = big[:, 6 * HS:10 * HS].rearrange("p (j t s) -> p j t s", j=GH, t=NT)
        names = ["xb", "xc", "sq", "v", "r", "t", "h", "h2", "q", "k", "vv", "d0", "d1", "d2", "den",
                 "y", "qq", "kk", "nv", "c", "nt", "res", "os", "oT", "ao", "g0", "g1", "g2", "g3",
                 "kv", "lat", "ngb", "w1e", "w2e", "evm", "ev2", "rest", "o1"]
        W = {n: big[:, i * S:(i + 1) * S] for i, n in enumerate(names)}
        assert len(names) <= 40
        pvs = sb("pvs", [P, 2, S])
        mx = sb("mx", [P, 4, NT])
        nb = sb("nb", [P, 4, NT])
        rec = sb("rec", [P, 2, NT * GH])
        ev = sb("ev", [32, 2, P])

        def bank(n):
            return ps[:, n, :]

        block = ctx.enter_context(nc.Block())

        def wait_apart(eng, s, value):
            if not isinstance(value, int):
                value = eng.to_reg(value)
            eng.wait_ge(sem("loaded"), LOADED)
            eng.wait_ge(s, value)

        def norm_pe(pe, ph, b, k):
            pe.wait_ge(sem(f"{ph}_x{k}"), b + 1)
            nc.tensor.matmul(bank(0), mean_w[:, :], W["xb"], start=True, stop=True)\
              .then_inc(sem(f"{ph}_mean{k}"), 1)
            pe.wait_ge(sem(f"{ph}_sq{k}"), b + 1)
            nc.tensor.matmul(bank(1), mean_w[:, :], W["sq"], start=True, stop=True)\
              .then_inc(sem(f"{ph}_var{k}"), 1)

        def norm_act(act, own, ph, b, k):
            act.wait_ge(sem(f"{ph}_xc{k}"), b + 1)
            nc.scalar.activation(W["sq"], W["xc"], ACT.Square).then_inc(sem(f"{ph}_sq{k}"), 1)
            act.wait_ge(sem(f"{ph}_v{k}"), b + 1)
            own(nc.scalar.activation(W["r"], W["v"], ACT.Ln))
            nc.scalar.activation(W["r"], W["r"], ACT.Exp, scale=-0.5).then_inc(sem(f"{ph}_r{k}"), 1)

        def newton(own, v, r, t):
            own(nc.vector.tensor_tensor(t, r, r, ALU.mult))
            own(nc.vector.tensor_tensor(t, t, v, ALU.mult))
            own(nc.vector.tensor_scalar(t, t, -0.5, 1.5, ALU.mult, ALU.add))
            own(nc.vector.tensor_tensor(r, r, t, ALU.mult))

        def norm_dve(dve, own, ph, b, k, shift, gain):
            dve.wait_ge(sem(f"{ph}_mean{k}"), b + 1)
            nc.vector.tensor_tensor(W["xc"], W["xb"], bank(0), ALU.subtract).then_inc(sem(f"{ph}_xc{k}"), 1)
            dve.wait_ge(sem(f"{ph}_var{k}"), b + 1)
            nc.vector.tensor_scalar(W["v"], bank(1), LN_EPS, None, ALU.add).then_inc(sem(f"{ph}_v{k}"), 1)
            dve.wait_ge(sem(f"{ph}_r{k}"), b + 1)
            newton(own, W["v"], W["r"], W["t"])
            own(nc.vector.tensor_tensor(W["h"], W["xc"], W["r"], ALU.mult))
            nc.vector.tensor_scalar(W["h"], W["h"], mb[:, gain:gain + 1], mb[:, shift:shift + 1],
                                    ALU.mult, ALU.add).then_inc(sem(f"{ph}_h{k}"), 1)

        def split(own, src, dst, done):
            own(nc.vector.tensor_copy(dst[:, 0, :], src))
            own(nc.vector.tensor_tensor(W["rest"], src, dst[:, 0, :], ALU.subtract))
            own(nc.vector.tensor_copy(dst[:, 1, :], W["rest"]))
            own(nc.vector.tensor_tensor(W["rest"], W["rest"], dst[:, 1, :], ALU.subtract))
            nc.vector.tensor_copy(dst[:, 2, :], W["rest"]).then_inc(done, 1)

        def store_parts(sp, ph, layer):
            with sp.Fori(0, B) as b:
                for o, (name, src, first) in enumerate((("pq", pq, 1), ("pk", pk, 2))):
                    sp.wait_ge(sem(f"{ph}_{name}"), b + first)
                    for a in range(SPLITS):
                        dst = parts[layer, o, bass.ds(b, 1), :, a, :, :].rearrange("o h d t -> (o h) d t")
                        sp.dma_start(dst, src[:, a, :]).then_inc(sem(f"{ph}_stored"), 16)
            sp.wait_ge(sem(f"{ph}_stored"), 16 + B * 2 * SPLITS * 16)

        def values_to_groups(own, b, n):
            by = bank(n).rearrange("p (t g j d) -> p g t j d", t=NT, g=NG, j=GH)
            for g in range(NG):
                own(nc.vector.tensor_copy(vall[:, bass.ds(b * NG + g, 1), :, :, 0:DH]
                                          .rearrange("p o t j d -> p (o t) j d"), by[:, g]))

        def batch_in_pool(pool, ph, b, done, with_out):
            wait_apart(pool, done, b + 1)
            nc.gpsimd.tensor_copy(mb[:, :], mod[:, bass.ds(b, 1), :].rearrange("p o m -> p (o m)"))\
              .then_inc(sem(f"{ph}_mb"), 1)
            nc.gpsimd.tensor_copy(W["xb"], x[:, bass.ts(b, S)]).then_inc(sem(f"{ph}_x0"), 1)
            if with_out:
                for g in range(NG):
                    nc.gpsimd.tensor_copy(
                        W["os"].rearrange("p (t g c) -> p t g c", t=NT, g=NG)[:, :, g, :],
                        oall[:, bass.ds(b * NG + g, 1), :, :].rearrange("p o t c -> p (o t) c"))\
                      .then_inc(sem(f"{ph}_os"), 1)

        def attn_out_pe(pe, ph, b, wo):
            pe.wait_ge(sem(f"{ph}_os"), b * NG + NG)
            for t in range(NT):
                last = nc.tensor.transpose(ps[:, 0, t * P:(t + 1) * P], W["os"][:, t * P:(t + 1) * P],
                                           ident[:, :])
            last.then_inc(sem(f"{ph}_oT"), 1)
            pe.wait_ge(sem(f"{ph}_oTs"), b + 1)
            nc.tensor.matmul(bank(1), wo[:, :], W["oT"], start=True, stop=True)\
              .then_inc(sem(f"{ph}_ao"), 1)

        def attn_out_dve(dve, own, ph, b, bias, gate):
            dve.wait_ge(sem(f"{ph}_oT"), b + 1)
            nc.vector.tensor_copy(W["oT"], bank(0)).then_inc(sem(f"{ph}_oTs"), 1)
            dve.wait_ge(sem(f"{ph}_mb"), b + 1)
            dve.wait_ge(sem(f"{ph}_x0"), b + 1)
            dve.wait_ge(sem(f"{ph}_ao"), b + 1)
            own(nc.vector.tensor_scalar(W["ao"], bank(1), bias, mb[:, gate:gate + 1], ALU.add, ALU.mult))
            nc.vector.tensor_tensor(W["xb"], W["xb"], W["ao"], ALU.add).then_inc(sem(f"{ph}_x1"), 1)

        def mlp_pe(pe, ph, b, n, up, down):
            def rise(u):
                if u >= 2:
                    pe.wait_ge(sem(f"{ph}_gelu"), b * n + (u - 1))
                nc.tensor.matmul(bank(4 + u % 2), up(u), W["h"], start=True, stop=True)\
                  .then_inc(sem(f"{ph}_up"), 1)
            rise(0)
            rise(1)
            for u in range(n):
                if u + 2 < n:
                    rise(u + 2)
                pe.wait_ge(sem(f"{ph}_gelu"), b * n + (u + 1))
                nc.tensor.matmul(bank(7), down(u), W[f"g{u % 4}"], start=(u == 0), stop=(u == n - 1))\
                  .then_inc(sem(f"{ph}_down"), 1)

        def mlp_act(act, ph, b, n, bias):
            for u in range(n):
                act.wait_ge(sem(f"{ph}_down"), b * n + (u + 1))
                act.wait_ge(sem(f"{ph}_up"), b * n + (u + 1))
                nc.scalar.activation(W[f"g{u % 4}"], bank(4 + u % 2), ACT.Gelu, bias=bias[:, u:u + 1])\
                  .then_inc(sem(f"{ph}_gelu"), 1)

        def each_slot(eng, L, slot):
            for s in range(UNROLL):
                slot(s, At(0), lambda n: n >= 0)
            with eng.Fori(1, HEADS // UNROLL) as i:
                at = At(i)
                for s in range(UNROLL):
                    slot(s, at, lambda n: True)
            end = At(HEADS // UNROLL)
            for s in range(LAG[L]):
                slot(s, end, lambda n: n < 0)

        def attn_sp(sp, L, layer):
            src_of = [parts[layer, o].rearrange("b (g j) a d t -> (b g) j a d t", g=NG) for o in range(2)]
            with sp.Fori(0, GROUPS // 2) as i:
                for g in range(2):
                    sp.wait_ge(sem(f"{L}_scores"), i * (4 * UNROLL // 2) + (8 * g + 1))
                    for a in range(SPLITS):
                        for r in range(SPLITS):
                            row = (a * SPLITS + r) * DH
                            for o, st, part in ((0, qst, r), (1, kst, a)):
                                src = src_of[o][bass.ds(i * 2 + g, 1), :, part, :, :]
                                sp.dma_start(st[row:row + DH, g, :, :], src.rearrange("o j d t -> d (o j) t"))\
                                  .then_inc(sem(f"{L}_stack{g}"), 16)

        def attn_pool(pool, L):
            with pool.Fori(0, GROUPS // 2) as i:
                for g in range(2):
                    wait_apart(pool, sem(f"{L}_pv"), i * 2 + (g + 1))
                    nc.gpsimd.tensor_copy(
                        vg[:, g, :, :, 0:VC],
                        vall[:, bass.ds(i * 2 + g, 1), :, :, :].rearrange("p o t j c -> p (o t) j c"))\
                      .then_inc(sem(f"{L}_vg"), 1)

        def attn_pe(pe, L, wait_read):
            def scores(n, at):
                par = (n // GH) % 2
                if n % GH == 0:
                    pe.wait_ge(sem(f"{L}_stack{par}"), at.turn * STACK + STACK)
                for c in range(2):
                    wait_read(n, c, at)
                    for t in (2 * c, 2 * c + 1):
                        last = nc.tensor.matmul(bank(t), qst[:, par, n % GH, t * P:(t + 1) * P],
                                                kst[:, par, n % GH, :], start=True, stop=True)
                    last.then_inc(sem(f"{L}_scores"), 1)

            def transposes(n, at):
                pe.wait_ge(sem(f"{L}_probs"), at.head + (n + 1))
                for kt in range(NT):
                    pe.wait_ge(sem(f"{L}_evac{kt % 2}"), at.head * 2 + (2 * n + kt // 2 + 1))
                    for t in range(NT):
                        last = nc.tensor.transpose(ps[:, 4 + kt % 2, t * P:(t + 1) * P],
                                                   Y[n % 4][:, t * S + kt * P:t * S + (kt + 1) * P], ident[:, :])
                    last.then_inc(sem(f"{L}_turned"), 1)

            def values(n, at):
                g, par = n // GH, (n // GH) % 2
                for k in range(2):
                    pe.wait_ge(sem(f"{L}_evac{k}"), at.head * 2 + (2 * n + 3))
                pe.wait_ge(sem(f"{L}_vg"), at.group + (g + 1))
                pe.wait_ge(sem(f"{L}_pvs"), at.group + (g + 1))
                for kt in range(NT):
                    for j in range(GH):
                        last = nc.tensor.matmul(ps[32 * j:32 * j + 32, 6, :], vg[:, par, kt, j, :], PT[:, j, kt, :],
                                                start=(kt == 0), stop=(kt == NT - 1))
                last.then_inc(sem(f"{L}_pv"), 1)
                pe.wait_ge(sem(f"{L}_pvs"), at.group + (g + 2))
                pe.wait_ge(sem(f"{L}_out"), at.group + (g + 1))
                for t in range(NT):
                    last = nc.tensor.transpose(ps[:, 7, t * P:(t + 1) * P], pvs[:, par, t * P:(t + 1) * P],
                                               ident[:, :])
                last.then_inc(sem(f"{L}_pvT"), 1)

            def slot(s, at, on):
                if on(s):
                    scores(s, at)
                n = s - LAG[L]
                if on(n):
                    transposes(n, at)
                    if n % GH == GH - 1:
                        values(n, at)
            each_slot(pe, L, slot)

        def group_out_dve(dve, L, n, at):
            g, par = n // GH, (n // GH) % 2
            dve.wait_ge(sem(f"{L}_pv"), at.group + (g + 1 + PV0))
            nc.vector.tensor_copy(pvs[:, par, :], bank(6)).then_inc(sem(f"{L}_pvs"), 1)
            dve.wait_ge(sem(f"{L}_pvT"), at.group + (g + 1))
            by = bank(7).rearrange("p (m c) -> p m c", c=32)
            nc.vector.reciprocal(rec[:, par, :], by[:, :, DH]).then_inc(sem(f"{L}_rec"), 1)
            dve.wait_ge(sem(f"{L}_rec"), at.group + (g + 1))
            dst = oall[:, bass.ds(at.group + g, 1), :, :].rearrange("p o t (j d) -> p (o t j) d", d=DH)
            nc.vector.tensor_tensor(dst, by[:, :, 0:DH],
                                    rec[:, par, :].unsqueeze(2).broadcast_to([P, NT * GH, DH]), ALU.mult)\
              .then_inc(sem(f"{L}_out"), 1)

        def attn1_act(act):
            def slot(s, at, on):
                if on(s):
                    act.wait_ge(sem("B_turned"), at.head * 4 + (4 * s + 1))
                    for c in range(2):
                        act.wait_ge(sem("B_scores"), at.head * 2 + (2 * s + c + 1 + SCORES0))
                        nc.scalar.activation(Y[s % 4][:, c * 2 * S:(c + 1) * 2 * S],
                                             ps[:, 2 * c:2 * c + 2, :].rearrange("p a s -> p (a s)"),
                                             ACT.Square).then_inc(sem("B_scored"), 1)
                n = s - 1
                if on(n):
                    act.wait_ge(sem("B_abs"), at.head + (n + 1))
                    nc.scalar.activation(A[n % 2], A[n % 2], ACT.Ln).then_inc(sem("B_ln"), 1)
                    act.wait_ge(sem("B_ln"), at.head + (n + 1))
                    nc.scalar.activation(A[n % 2], A[n % 2], ACT.Exp, scale=-2.0).then_inc(sem("B_inv"), 1)
                n = s - 2
                if on(n):
                    act.wait_ge(sem("B_bias"), at.head + (n + 1))
                    for t in range(NT):
                        sl = Y[n % 4][:, t * S:(t + 1) * S]
                        last = nc.scalar.activation(sl, sl, ACT.Exp, bias=nb[:, n % 4, t:t + 1], scale=0.5)
                    last.then_inc(sem("B_probs"), 1)
            each_slot(act, "B", slot)

        def attn1_dve(dve):
            def slot(s, at, on):
                if on(s):
                    dve.wait_ge(sem("B_scored"), at.head * 2 + (2 * s + 4))
                    nc.vector.tensor_scalar(Y[s % 4], Y[s % 4], 1.0, ZERO_GUARD, ALU.subtract, ALU.subtract)\
                      .then_inc(sem("B_den"), 1)
                    dve.wait_ge(sem("B_den"), at.head + (s + 1))
                    nc.vector.tensor_scalar(A[s % 2].bitcast(U32), Y[s % 4].bitcast(U32), 0x7fffffff, None,
                                            ALU.bitwise_and).then_inc(sem("B_abs"), 1)
                n = s - 3
                if on(n):
                    for kt in range(NT):
                        dve.wait_ge(sem("B_turned"), at.head * 4 + (4 * n + kt + 1 + TURNED0))
                        nc.vector.tensor_copy(PT[:, n % GH, kt, :], bank(4 + kt % 2))\
                          .then_inc(sem(f"B_evac{kt % 2}"), 1)
                    if n % GH == GH - 1:
                        group_out_dve(dve, "B", n, at)
                n = s - 1
                if on(n):
                    wait_apart(dve, sem("B_inv"), at.head + (n + 1))
                    for t in range(NT):
                        sl = slice(t * S, (t + 1) * S)
                        nc.vector.tensor_tensor_reduce(out=Y[n % 4][:, sl], in0=Y[n % 4][:, sl], in1=A[n % 2][:, sl],
                                                       scale=-1.0, scalar=-3e38, op0=ALU.mult, op1=ALU.max,
                                                       accum_out=mx[:, n % 4, t:t + 1]).then_inc(sem("B_quot"), 1)
                    dve.wait_ge(sem("B_quot"), at.head * 4 + (4 * n + 4))
                    nc.vector.tensor_scalar(nb[:, n % 4, :], mx[:, n % 4, :], -0.5, None, ALU.mult)\
                      .then_inc(sem("B_bias"), 1)
            each_slot(dve, "B", slot)

        def attn2_act(act):
            def slot(s, at, on):
                for t in range(NT):
                    n = s - 1
                    if on(n):
                        if t == 0:
                            act.wait_ge(sem("D_bias"), at.head + (n + 1))
                        sl = Y[n % 4][:, t * S:(t + 1) * S]
                        ins = nc.scalar.activation(sl, sl, ACT.Exp, bias=nb[:, n % 4, t:t + 1], scale=DOT_SCALE)
                        if t == NT - 1:
                            ins.then_inc(sem("D_probs"), 1)
                    n = s - 2
                    if on(n) and t % 2:
                        act.wait_ge(sem("D_turned"), at.head * 4 + (4 * n + t + 1 + TURNED0))
                        nc.scalar.activation(PT[:, n % GH, t, :], bank(5), ACT.Copy)\
                          .then_inc(sem("D_evac1"), 1)
            each_slot(act, "D", slot)

        def attn2_dve(dve):
            def slot(s, at, on):
                for t in range(NT):
                    if on(s):
                        if t == 0:
                            dve.wait_ge(sem("D_turned"), at.head * 4 + (4 * s + 1))
                        wait_apart(dve, sem("D_scores"), at.head * 2 + (2 * s + t // 2 + 1 + SCORES0))
                        nc.vector.tensor_tensor_reduce(out=Y[s % 4][:, t * S:(t + 1) * S], in0=bank(t),
                                                       in1=decay[:, t, :],
                                                       scale=1.0, scalar=-3e38, op0=ALU.mult, op1=ALU.max,
                                                       accum_out=mx[:, s % 4, t:t + 1]).then_inc(sem("D_quot"), 1)
                    n = s - 2
                    if on(n) and t % 2 == 0:
                        dve.wait_ge(sem("D_turned"), at.head * 4 + (4 * n + t + 1 + TURNED0))
                        nc.vector.tensor_copy(PT[:, n % GH, t, :], bank(4)).then_inc(sem("D_evac0"), 1)
                if on(s):
                    dve.wait_ge(sem("D_quot"), at.head * 4 + (4 * s + 4 + 3))
                    nc.vector.tensor_scalar(nb[:, s % 4, :], mx[:, s % 4, :], -DOT_SCALE, None, ALU.mult)\
                      .then_inc(sem("D_bias"), 1)
                if on(n) and n % GH == GH - 1:
                    group_out_dve(dve, "D", n, at)
            each_slot(dve, "D", slot)

        loads = [(x[:, :], xT), (c_sb[:, :, :], cT), (wmod_sb[:, :, :], wmod), (mean_w[:, :], blk_in[:, 0, :]),
                 (ident[:, :], ident_in), (blk[:, :], blk_in[:, 1, :]), (ones[:, :], blk_in[:, 2, :]),
                 (w_qkv[:, :, :], wqkv), (b_qkv[:, :], bqkv), (al[:, :], alpha.partition_broadcast(P)),
                 (decay[:, :, :], decay_in), (wo0_sb[:, :], wo0), (bo0_sb[:, :], bo0), (gw_sb[:, :], gwT),
                 (gb_sb[:, :], gb.partition_broadcast(P)), (rms_sb[:, :], rms.partition_broadcast(P)),
                 (w1_sb[:, :, :], w1), (b1_sb[:, :], b1), (w2_sb[:, :, :], w2), (b2_sb[:, :], b2),
                 (l1w_sb[:, :, :], l1w), (dn_sb[:, :], l1down), (up_sb[:, :, :], l1up), (wo1_sb[:, :], l1wo),
                 (mw1_sb[:, :], mw1), (mb1_sb[:, :], mb1), (mw2_sb[:, :, :], mw2), (mb2_sb[:, :], mb2),
                 (sc_sb[:, :], scale.partition_broadcast(P))]
        LOADED = 16 * len(loads)

        @block.sync
        def _(sp):
            for dst, src in loads:
                sp.dma_start(dst, src).then_inc(sem("loaded"), 16)
            store_parts(sp, "A", 0)
            sp.wait_ge(sem("zeros"), 3)
            attn_sp(sp, "B", 0)
            store_parts(sp, "C", 1)
            attn_sp(sp, "D", 1)
            with sp.Fori(0, B) as b:
                sp.wait_ge(sem("E_res"), b + 2)
                sp.dma_start(out[:, bass.ts(b, S)], W["res"]).then_inc(sem("E_outd"), 16)
            sp.wait_ge(sem("E_outd"), 16 + 16 * B)

        @block.gpsimd
        def _(pool):
            first = (("A_pk", 1), ("C_pk", 1), ("E_res", 1), ("A_stored", 16), ("C_stored", 16), ("E_outd", 16),
                     ("C_down", DOWN0), ("E_down", DOWN0), ("B_scored", 2), ("D_quot", 3),
                     ("B_turned", TURNED0), ("D_turned", TURNED0), ("B_scores", SCORES0), ("D_scores", SCORES0),
                     ("B_pv", PV0), ("D_pv", PV0), ("B_pvs", 1), ("D_pvs", 1), ("B_out", 1), ("D_out", 1),
                     ("B_evac0", 1), ("B_evac1", 1), ("D_evac0", 1), ("D_evac1", 1))
            for i, (name, n) in enumerate(first):
                nc.gpsimd.memset(small[:, i:i + 1], 0.0).then_inc(sem(name), n)
            nc.gpsimd.memset(s_base[:, :], YAT_BASE).then_inc(sem("base"), 1)
            nc.gpsimd.memset(vg[:, :, :, :, :], 0.0).then_inc(sem("zeros"), 1)
            nc.gpsimd.memset(vall[:, :, :, :, DH:VC], 1.0).then_inc(sem("zeros"), 1)
            pool.wait_ge(sem("loaded"), LOADED)
            pool.wait_ge(sem("base"), 1)
            nc.gpsimd.tensor_tensor(s_yat[:, :], s_base[:, :], al[:, :], ALU.pow).then_inc(sem("yat"), 1)
            pool.wait_ge(sem("mod"), 1)
            with pool.Fori(0, B) as b:
                batch_in_pool(pool, "A", b, sem("A_pk"), False)
            pool.wait_ge(sem("A_pk"), B + 1)
            pool.wait_ge(sem("zeros"), 3)
            attn_pool(pool, "B")
            pool.wait_ge(sem("B_out"), GROUPS + 1)
            with pool.Fori(0, B) as b:
                batch_in_pool(pool, "C", b, sem("C_pk"), True)
                wait_apart(pool, sem("C_x2"), b + 1)
                nc.gpsimd.tensor_copy(x[:, bass.ts(b, S)], W["xb"]).then_inc(sem("C_xst"), 1)
            pool.wait_ge(sem("C_pk"), B + 1)
            attn_pool(pool, "D")
            pool.wait_ge(sem("D_out"), GROUPS + 1)
            with pool.Fori(0, B) as b:
                batch_in_pool(pool, "E", b, sem("E_res"), True)

        def first_guess(act, own, ready, v, r, done, b):
            act.wait_ge(ready, b + 1)
            own(nc.scalar.activation(r, v, ACT.Ln))
            nc.scalar.activation(r, r, ACT.Exp, scale=-0.5).then_inc(done, 1)

        @block.scalar
        def _(act):
            act.wait_ge(sem("loaded"), LOADED)
            nc.scalar.preload_act_table_set("natural_log_exp_and_others")
            nc.scalar.activation(sil[:, 0], c_sb[:, :, :], ACT.Exp, scale=-1.0).then_inc(sem("sil_e"), 1)
            with act.Fori(0, B) as b:
                own = Order(act, sem("A_act"), b * OWN["actA"])
                norm_act(act, own, "A", b, 0)
                act.wait_ge(sem("A_h0"), b + 1)
                nc.scalar.activation(W["h2"], W["h"], ACT.Square).then_inc(sem("A_h2"), 1)
                act.wait_ge(sem("A_dot"), b + 1)
                for j in range(3):
                    nc.scalar.activation(W[f"d{j}"], bank(2 + j), ACT.Square).then_inc(sem("A_d2"), 1)
                act.wait_ge(sem("A_q"), b + 1)
                nc.scalar.activation(W["qq"], W["q"], ACT.Square).then_inc(sem("A_qq"), 1)
                act.wait_ge(sem("A_k"), b + 1)
                nc.scalar.activation(W["kk"], W["k"], ACT.Square).then_inc(sem("A_qq"), 1)
                first_guess(act, own, sem("A_nv"), W["nv"], W["c"], sem("A_c"), b)
                assert own.n == OWN["actA"]
            attn1_act(act)
            with act.Fori(0, B) as b:
                own = Order(act, sem("C_act"), b * OWN["actC"])
                norm_act(act, own, "C", b, 1)
                first_guess(act, own, sem("C_ms"), small[:, 32:36], small[:, 36:40], sem("C_rms"), b)
                act.wait_ge(sem("C_lm"), b + 1)
                nc.scalar.activation(W["t"][:, 32:64], W["t"][:, 0:32], ACT.Exp, scale=2.0).then_inc(sem("C_le"), 1)
                mlp_act(act, "C", b, EU, b1_sb)
                norm_act(act, own, "C", b, 2)
                assert own.n == OWN["actC"]
            attn2_act(act)
            with act.Fori(0, B) as b:
                own = Order(act, sem("E_act"), b * OWN["actE"])
                norm_act(act, own, "E", b, 1)
                mlp_act(act, "E", b, MU, mb1_sb)
                assert own.n == OWN["actE"]

        @block.tensor
        def _(pe):
            pe.wait_ge(sem("sil"), 1)
            for l in range(2):
                for m in range(6):
                    last = nc.tensor.matmul(ps[:, 0, (6 * l + m) * B:(6 * l + m + 1) * B],
                                            wmod_sb[:, l, m * D:(m + 1) * D], sil[:, 3, l, :], start=True, stop=True)
            last.then_inc(sem("modps"), 1)
            pe.wait_ge(sem("wsq"), 1)
            for j in range(3):
                last = nc.tensor.matmul(ps[:, 1, j:j + 1], W["d0"][:, j * D:(j + 1) * D], ones[:, 0:1],
                                        start=True, stop=True)
            last.then_inc(sem("wn"), 1)
            pe.wait_ge(sem("wns"), 1)
            with pe.Fori(0, B) as b:
                norm_pe(pe, "A", b, 0)
                pe.wait_ge(sem("A_h0"), b + 1)
                for j in range(3):
                    last = nc.tensor.matmul(bank(2 + j), w_qkv[:, j, :], W["h"], start=True, stop=True)
                last.then_inc(sem("A_dot"), 1)
                pe.wait_ge(sem("A_h2"), b + 1)
                nc.tensor.matmul(bank(5), ones[:, :], W["h2"], start=True, stop=True).then_inc(sem("A_n2"), 1)
                pe.wait_ge(sem("A_s2"), b + 1)
                nc.tensor.matmul(bank(6), blk[:, :], W["qq"], start=True, stop=True).then_inc(sem("A_nn"), 1)
                pe.wait_ge(sem("A_v"), b + 1)
                for t in range(NT):
                    last = nc.tensor.transpose(ps[:, 7, t * P:(t + 1) * P], W["vv"][:, t * P:(t + 1) * P], ident[:, :])
                last.then_inc(sem("A_vt"), 1)
            pe.wait_ge(sem("zeros"), 3)
            attn_pe(pe, "B", lambda n, c, at: pe.wait_ge(sem("B_scored"), at.head * 2 + (2 * n + c + 1)))
            with pe.Fori(0, B) as b:
                attn_out_pe(pe, "C", b, wo0_sb)
                norm_pe(pe, "C", b, 1)
                pe.wait_ge(sem("C_h1"), b + 1)
                for t in range(NT):
                    last = nc.tensor.matmul(ps[:, 2, t * EX:(t + 1) * EX], W["h"][:, t * P:(t + 1) * P], gw_sb[:, :],
                                            start=True, stop=True)
                last.then_inc(sem("C_lg"), 1)
                pe.wait_ge(sem("C_ng"), b + 1)
                for t in range(NT):
                    last = nc.tensor.matmul(ps[:, 3, t * P:(t + 1) * P],
                                            small[:, 44 + t:45 + t].broadcast_to([P, P]), ident[:, :],
                                            start=True, stop=True)
                last.then_inc(sem("C_ngb"), 1)
                mlp_pe(pe, "C", b, EU, lambda u: w1_sb[:, u, :], lambda u: w2_sb[:, u, :])
                norm_pe(pe, "C", b, 2)
                pe.wait_ge(sem("C_h2"), b + 1)
                nc.tensor.matmul(bank(2), l1w_sb[:, 0, :], W["h"], start=True, stop=True)
                nc.tensor.matmul(bank(3), l1w_sb[:, 1, :], W["h"], start=True, stop=False)
                nc.tensor.matmul(bank(3), l1w_sb[:, 2, :], W["h"], start=False, stop=True).then_inc(sem("C_kv"), 1)
                pe.wait_ge(sem("C_kvs"), b + 1)
                nc.tensor.matmul(ps[0:32, 4, :], dn_sb[:, :], W["kv"], start=True, stop=True).then_inc(sem("C_lat"), 1)
                pe.wait_ge(sem("C_lats"), b + 1)
                nc.tensor.matmul(bank(5), up_sb[:, 0, :], W["lat"][0:32, :], start=True, stop=True)
                for t in range(NT):
                    last = nc.tensor.matmul(ps[:, 6, t * P:(t + 1) * P], W["lat"][0:32, t * P:(t + 1) * P],
                                            up_sb[:, 1, :], start=True, stop=True)
                last.then_inc(sem("C_rec"), 1)
            attn_pe(pe, "D", lambda n, c, at: pe.wait_ge(sem("D_quot"), at.head * 4 + (4 * n + 2 * c + 1)))
            with pe.Fori(0, B) as b:
                attn_out_pe(pe, "E", b, wo1_sb)
                norm_pe(pe, "E", b, 1)
                pe.wait_ge(sem("E_h1"), b + 1)
                for k in range(2):
                    last = nc.tensor.transpose(ps[0:32, 2, k * P:(k + 1) * P], W["h"][:, 1 + k:33 + k], ident[:, :])
                last.then_inc(sem("E_rows"), 1)
                pe.wait_ge(sem("E_ev"), b + 1)
                nc.tensor.matmul(bank(3), ev[:, 1, :], W["evm"][0:32, :], start=True, stop=True)
                for t in range(MU):
                    last = nc.tensor.matmul(ps[:, 6, t * P:(t + 1) * P], ev[:, 1, :],
                                            W["ev2"][0:32, t * P:(t + 1) * P], start=True, stop=True)
                last.then_inc(sem("E_delta"), 1)
                pe.wait_ge(sem("E_weights"), b + 1)
                mlp_pe(pe, "E", b, MU, lambda u: W["w1e"][:, u * P:(u + 1) * P],
                       lambda u: W["w2e"][:, u * P:(u + 1) * P])

        @block.vector
        def _(dve):
            nc.vector.memset(qst[:, :, :, :], 0.0).then_inc(sem("clear"), 1)
            nc.vector.memset(kst[:, :, :, :], 0.0).then_inc(sem("zeros"), 1)
            dve.wait_ge(sem("loaded"), LOADED)
            own = Order(dve, sem("P_dve"), 0)
            dve.wait_ge(sem("sil_e"), 1)
            own(nc.vector.tensor_scalar(sil[:, 1], sil[:, 0], 1.0, None, ALU.add))
            own(nc.vector.reciprocal(sil[:, 2], sil[:, 1]))
            nc.vector.tensor_tensor(sil[:, 3], c_sb[:, :, :], sil[:, 2], ALU.mult).then_inc(sem("sil"), 1)
            nc.vector.tensor_tensor(W["d0"][:, 0:3 * D].rearrange("p (j d) -> p j d", j=3), w_qkv[:, :, :],
                                    w_qkv[:, :, :], ALU.mult).then_inc(sem("wsq"), 1)
            dve.wait_ge(sem("modps"), 1)
            own(nc.vector.tensor_copy(mod[:, :, :].rearrange("p b m -> p m b"),
                                      ps[:, 0, 0:12 * B].rearrange("p (m b) -> p m b", b=B)))
            for m in (CA, CB, 6 + CA, 6 + CB):
                own(nc.vector.tensor_scalar(mod[:, :, m], mod[:, :, m], 1.0, None, ALU.add))
            for m in (GA, GB, 6 + GA, 6 + GB):
                g, size, sign = mod[:, :, m], small[:, 64:64 + B], small[:, 80:80 + B]
                own(nc.vector.tensor_scalar(size, g, -1.0, 0.25, ALU.mult, ALU.max))
                own(nc.vector.tensor_tensor(size, size, g, ALU.max))
                own(nc.vector.tensor_scalar(sign, g, 0.0, 2.0, ALU.is_ge, ALU.mult))
                own(nc.vector.tensor_scalar(sign, sign, -1.0, None, ALU.add))
                own(nc.vector.tensor_tensor(g, size, sign, ALU.mult))
            dve.wait_ge(sem("wn"), 1)
            own(nc.vector.tensor_scalar(wn[:, :], ps[:, 1, 0:3], ATT_EPS, None, ALU.add))
            own(nc.vector.reduce_sum(b2s[:, :], b2_sb[:, :], axis=AX_X))
            dve.wait_ge(sem("yat"), 1)
            nc.vector.memset(small[:, 96:97], 0.0).then_inc(sem("mod"), 1)
            nc.vector.memset(small[:, 97:98], 0.0).then_inc(sem("wns"), 1)

            with dve.Fori(0, B) as b:
                own = Order(dve, sem("A_dve"), b * OWN["dveA"])
                dve.wait_ge(sem("A_mb"), b + 1)
                norm_dve(dve, own, "A", b, 0, SA, CA)
                dve.wait_ge(sem("A_n2"), b + 1)
                dve.wait_ge(sem("A_d2"), b * 3 + 3)
                for j, (dst, done) in enumerate((("q", "A_q"), ("k", "A_k"), ("vv", "A_v"))):
                    own(nc.vector.tensor_scalar(W["den"], bank(5), wn[:, j:j + 1], None, ALU.add))
                    own(nc.vector.scalar_tensor_tensor(W["y"], bank(2 + j), -2.0, W["den"], ALU.mult, ALU.add))
                    own(nc.vector.reciprocal(W["den"], W["y"]))
                    own(nc.vector.tensor_tensor(W["y"], W[f"d{j}"], W["den"], ALU.mult))
                    nc.vector.tensor_scalar(W[dst], W["y"], b_qkv[:, j:j + 1], s_yat[:, j:j + 1],
                                            ALU.add, ALU.mult).then_inc(sem(done), 1)
                dve.wait_ge(sem("A_qq"), b * 2 + 2)
                nc.vector.tensor_tensor(W["qq"], W["qq"], W["kk"], ALU.add).then_inc(sem("A_s2"), 1)
                dve.wait_ge(sem("A_nn"), b + 1)
                nc.vector.tensor_scalar(W["nv"], bank(6), ATT_EPS, 0.5, ALU.add, ALU.mult)\
                  .then_inc(sem("A_nv"), 1)
                dve.wait_ge(sem("A_vt"), b + 1)
                values_to_groups(own, b, 7)
                dve.wait_ge(sem("A_c"), b + 1)
                newton(own, W["nv"], W["c"], W["nt"])
                own(nc.vector.tensor_tensor(W["q"], W["q"], W["c"], ALU.mult))
                dve.wait_ge(sem("A_stored"), b * (2 * SPLITS * 16) + 16)
                split(own, W["q"], pq, sem("A_pq"))
                dve.wait_ge(sem("A_pq"), b + 1)
                split(own, W["k"], pk, sem("A_pk"))
                assert own.n == OWN["dveA"]
            attn1_dve(dve)
            with dve.Fori(0, B) as b:
                own = Order(dve, sem("C_dve"), b * OWN["dveC"])
                attn_out_dve(dve, own, "C", b, bo0_sb[:, 0:1], GA)
                norm_dve(dve, own, "C", b, 1, SB, CB)
                lg = W["t"][:, 0:32].rearrange("p (t e) -> p t e", e=EX)
                l2 = W["t"][:, 32:64].rearrange("p (t e) -> p t e", e=EX)
                by_expert = lambda v: v[:, :].unsqueeze(1).broadcast_to([P, NT, EX])
                by_token = lambda c: small[:, c:c + NT].unsqueeze(2).broadcast_to([P, NT, EX])
                dve.wait_ge(sem("C_lg"), b + 1)
                own(nc.vector.tensor_tensor(lg, ps[:, 2, 0:32].rearrange("p (t e) -> p t e", e=EX),
                                            by_expert(gb_sb), ALU.add))
                own(nc.vector.tensor_tensor(l2, lg, lg, ALU.mult))
                own(nc.vector.reduce_sum(small[:, 40:44], l2, axis=AX_X))
                nc.vector.tensor_scalar(small[:, 32:36], small[:, 40:44], 1 / EX, RMS_EPS, ALU.mult, ALU.add)\
                  .then_inc(sem("C_ms"), 1)
                dve.wait_ge(sem("C_rms"), b + 1)
                newton(own, small[:, 32:36], small[:, 36:40], small[:, 48:52])
                own(nc.vector.tensor_tensor(lg, lg, by_token(36), ALU.mult))
                own(nc.vector.tensor_tensor(lg, lg, by_expert(rms_sb), ALU.mult))
                own(nc.vector.reduce_max(small[:, 40:44], lg, axis=AX_X))
                nc.vector.tensor_tensor(lg, lg, by_token(40), ALU.subtract).then_inc(sem("C_lm"), 1)
                dve.wait_ge(sem("C_le"), b + 1)
                own(nc.vector.reduce_sum(small[:, 48:52], l2, axis=AX_X))
                own(nc.vector.tensor_scalar(small[:, 48:52], small[:, 48:52], NORM_EPS, 1.0, ALU.mult, ALU.add))
                nc.vector.reciprocal(small[:, 44:48], small[:, 48:52]).then_inc(sem("C_ng"), 1)
                dve.wait_ge(sem("C_ngb"), b + 1)
                own(nc.vector.tensor_copy(W["ngb"], bank(3)))
                dve.wait_ge(sem("C_down"), b * EU + (EU + DOWN0))
                own(nc.vector.tensor_scalar(W["y"], bank(7), b2s[:, 0:1], None, ALU.add))
                own(nc.vector.tensor_tensor(W["y"], W["y"], W["ngb"], ALU.mult))
                nc.vector.scalar_tensor_tensor(W["xb"], W["y"], mb[:, GB:GB + 1], W["xb"], ALU.mult, ALU.add)\
                  .then_inc(sem("C_x2"), 1)
                norm_dve(dve, own, "C", b, 2, 6 + SA, 6 + CA)
                dve.wait_ge(sem("C_kv"), b + 1)
                nc.vector.tensor_copy(W["kv"], bank(3)).then_inc(sem("C_kvs"), 1)
                dve.wait_ge(sem("C_lat"), b + 1)
                nc.vector.tensor_copy(W["lat"][0:32, :], ps[0:32, 4, :]).then_inc(sem("C_lats"), 1)
                dve.wait_ge(sem("C_xst"), b + 1)
                dve.wait_ge(sem("C_stored"), b * (2 * SPLITS * 16) + 16)
                split(own, bank(2), pq, sem("C_pq"))
                dve.wait_ge(sem("C_pq"), b + 1)
                dve.wait_ge(sem("C_rec"), b + 1)
                values_to_groups(own, b, 6)
                split(own, bank(5), pk, sem("C_pk"))
                assert own.n == OWN["dveC"]
            attn2_dve(dve)
            with dve.Fori(0, B) as b:
                own = Order(dve, sem("E_dve"), b * OWN["dveE"])
                attn_out_dve(dve, own, "E", b, 0.0, 6 + GA)
                norm_dve(dve, own, "E", b, 1, 6 + SB, 6 + CB)
                dve.wait_ge(sem("E_rows"), b + 1)
                own(nc.vector.tensor_copy(ev[:, :, :], ps[0:32, 2, 0:2 * P].rearrange("p (k c) -> p k c", k=2)))
                for i in range(MU):
                    own(nc.vector.tensor_scalar(W["evm"][0:32, i * P:(i + 1) * P], ev[:, 0, :],
                                                ident[0:32, 2 * i:2 * i + 1], None, ALU.mult))
                turned = ev[:, 0, :].rearrange("p (r t) -> p t r", t=MU)
                for i in range(MU):
                    dst = W["ev2"][0:32, :].rearrange("p (t i r) -> p t i r", t=MU, i=MU)[:, :, i, :]
                    ins = nc.vector.tensor_scalar(dst, turned, ident[0:32, 2 * MU + 2 * i:2 * MU + 2 * i + 1],
                                                  None, ALU.mult)
                    if i < MU - 1:
                        own(ins)
                    else:
                        ins.then_inc(sem("E_ev"), 1)
                dve.wait_ge(sem("E_delta"), b + 1)
                own(nc.vector.scalar_tensor_tensor(W["w1e"], bank(3), sc_sb[:, 0:1], mw1_sb[:, :], ALU.mult, ALU.add))
                nc.vector.scalar_tensor_tensor(W["w2e"], bank(6), sc_sb[:, 0:1],
                                               mw2_sb[:, :, :].rearrange("p u d -> p (u d)"), ALU.mult, ALU.add)\
                  .then_inc(sem("E_weights"), 1)
                dve.wait_ge(sem("E_down"), b * MU + (MU + DOWN0))
                own(nc.vector.tensor_scalar(W["y"], bank(7), mb2_sb[:, 0:1], mb[:, 6 + GB:7 + GB], ALU.add, ALU.mult))
                dve.wait_ge(sem("E_outd"), b * 16 + 16)
                nc.vector.tensor_tensor(W["res"], W["y"], W["xb"], ALU.add).then_inc(sem("E_res"), 1)
                assert own.n == OWN["dveE"]


def kernel(**inputs):
    import concourse.bacc as bacc
    from concourse.bass_utils import run_bass_kernel_spmd

    a = {k: np.asarray(v) for k, v in inputs.items()}
    col = lambda v: np.ascontiguousarray(v.reshape(-1, 1))
    d = np.arange(D)
    i = np.arange(S, dtype=np.float32)
    decay = np.exp(-np.float32(0.01) * np.abs(i[:, None] - i[None, :])).astype(np.float32)
    consts = np.stack([np.full((D, D), 1 / D), d[:, None] // DH == d[None, :] // DH, np.ones((D, D))],
                      axis=1).astype(np.float32)
    lay = {
        "xT": a["L0_attn_inputs_q"].reshape(B * S, D).T,
        "cT": np.stack([a["L0_c"].T, a["L1_c"].T], axis=1),
        "wmod": np.stack([a["L0_wmod"], a["L1_wmod"]], axis=1),
        "wqkv": np.stack([a["L0_attn_wq"], a["L0_attn_wk"], a["L0_attn_wv"]], axis=1),
        "bqkv": np.stack([a["L0_attn_bq"], a["L0_attn_bk"], a["L0_attn_bv"]], axis=1),
        "alpha": np.concatenate([a["L0_attn_aq"], a["L0_attn_ak"], a["L0_attn_av"]]),
        "wo0": a["L0_attn_wo"], "bo0": col(a["L0_attn_bo"]),
        "gwT": a["L0_ffn_gate_w"].T, "gb": a["L0_ffn_gate_b"], "rms": a["L0_ffn_rms_w"],
        "w1": a["L0_ffn_w1"].transpose(1, 0, 2).reshape(D, EU, P),
        "b1": a["L0_ffn_b1"].reshape(EU, P).T,
        "w2": a["L0_ffn_w2"].reshape(EU, P, D).transpose(1, 0, 2),
        "b2": a["L0_ffn_b2"].T,
        "l1w": np.stack([a["L1_attn_W_q"], a["L1_attn_W_k"], a["L1_attn_W_v"]], axis=1),
        "l1down": a["L1_attn_W_down_kv"],
        "l1up": np.stack([a["L1_attn_W_up_k"], a["L1_attn_W_up_v"]], axis=1),
        "l1wo": a["L1_attn_W_o"],
        "mw1": a["L1_ffn_W1"].T, "mb1": a["L1_ffn_b1"].reshape(MU, P).T,
        "mw2": a["L1_ffn_W2"].T.reshape(MU, P, D).transpose(1, 0, 2), "mb2": col(a["L1_ffn_b2"]),
        "scale": a["L1_ffn_scale"].reshape(1),
        "ident_in": np.eye(P, dtype=np.float32),
        "blk_in": consts,
        "decay_in": decay.reshape(NT, P, S).transpose(1, 0, 2),
    }
    nc = bacc.Bacc("TRN2", target_bir_lowering=False, num_devices=1)
    arrays, args = {}, {}
    for name, v in lay.items():
        arrays[f"in_{name}"] = np.ascontiguousarray(v)
        args[name] = nc.dram_tensor(f"in_{name}", v.shape, mybir.dt.from_np(v.dtype), kind="ExternalInput").ap()
    parts = nc.dram_tensor("parts", (2, 2, B, H, SPLITS, DH, S), BF16, kind="Internal").ap()
    out = nc.dram_tensor("out_0", (D, B * S), F32, kind="ExternalOutput").ap()
    build(nc, parts=parts, out=out, **args)
    r = run_bass_kernel_spmd(nc, [arrays], core_ids=[0])
    return np.ascontiguousarray(r.results[0]["out_0"].T).reshape(B, S, D)
```

```python
import math
from itertools import zip_longest
from contextlib import ExitStack

import numpy as np
import concourse.bass as bass
from concourse import mybir

F32 = mybir.dt.float32
BF16 = mybir.dt.bfloat16
U32 = mybir.dt.uint32
ALU = mybir.AluOpType
ACT = mybir.ActivationFunctionType
AX_X = mybir.AxisListType.X

B, S, D = 8, 512, 128
H, DH = 16, 8
P = 128
NT = S // P
GH = 4
NG = H // GH
GROUPS = B * NG
HEADS = B * H
SPLITS = 3
KROWS = SPLITS * SPLITS * DH
VC = DH + 1
EX, HID = 8, 256
EU = EX * HID // P
MH = 512
MU = MH // P
LN_EPS = 1e-5
ATT_EPS = 1e-5
RMS_EPS = float(np.finfo(np.float32).eps)
NORM_EPS = 1e-6
YAT_BASE = math.sqrt(D) / math.log(1 + D)
DOT_SCALE = 1 / math.sqrt(D)
ZERO_GUARD = 1e-12
SA, CA, GA, SB, CB, GB = range(6)
LAYER = {"B": 0, "D": 1}
LAG = {"B": 3, "D": 2}
UNROLL = 8
OUT_LAG = 7
FILL = 2
PAIR = 2
TURNS = B // PAIR


class Order:

    def __init__(self, eng, sem, base):
        self.eng, self.sem, self.base, self.n = eng, sem, base, 0

    def __call__(self, ins):
        self.n += 1
        ins.then_inc(self.sem, 1)
        self.eng.wait_ge(self.sem, self.base + self.n)


OWN = {"dveA": 34, "dveC": 38, "dveE": 16, "actA": 2, "actC": 3, "actE": 1}


def own_base(eng, ph, i):
    before = sum(OWN[eng + q] * TURNS for q in "ACE"[:"ACE".index(ph)])
    return i * OWN[eng + ph] + before


SCORES0 = 2 * GH * 2 - 7
TURNED0 = 13
QUOT0 = 3
PV0 = 2
DOWN0 = 4
STACK = 2 * SPLITS * SPLITS * 16


class At:

    def __init__(self, turn, L):
        self.place = turn * 2
        self.turn = turn + LAYER[L] * (HEADS // UNROLL)
        self.group, self.head = self.turn * 2, self.turn * UNROLL


def build(nc, xT, cT, wmod, wqkv, bqkv, alpha, wo0, bo0, gwT, gb, rms, w1, b1, w2, b2,
          l1w, l1down, l1up, l1wo, mw1, mb1, mw2, mb2, scale, ident_in, blk_in, decay_in,
          parts, x1, out):
    ctx = ExitStack()
    with ctx:
        def sb(name, shape, dt=F32):
            return ctx.enter_context(nc.sbuf_tensor(name, shape, dt))

        sems = {}

        def sem(name):
            if name not in sems:
                sems[name] = ctx.enter_context(nc.semaphore(name))
            return sems[name]

        vall = sb("vall", [P, GROUPS, NT, GH, VC])
        vg = sb("vg", [P, 2, NT, GH, 32])
        oall = sb("oall", [P, GROUPS, NT, GH * DH])
        qst = sb("qst", [P, 2, GH, S], BF16)
        kst = sb("kst", [P, 2, GH, S], BF16)
        decay = sb("decay", [P, NT, S])
        big = sb("big", [P, 56 * S])
        small = sb("small", [P, 64])
        mod = sb("mod", [P, B, 12])
        mbs = sb("mbs", [P, PAIR, 12])
        ident = sb("ident", [P, P])
        mean_w = sb("mean_w", [P, P])
        ones = sb("ones", [P, P])
        blk = sb("blk", [P, P])
        wmod_sb = big[:, 46 * S:49 * S].rearrange("p (l m) -> p l m", l=2)
        c_sb = sb("c_sb", [P, 2, B])
        sil = sb("sil", [P, 4, 2, B])
        w_qkv = sb("w_qkv", [P, 3, D])
        b_qkv = sb("b_qkv", [P, 3])
        al = sb("al", [P, 3])
        s_base = sb("s_base", [P, 3])
        s_yat = sb("s_yat", [P, 3])
        wn = sb("wn", [P, 3])
        wo0_sb = sb("wo0_sb", [P, D])
        bo0_sb = sb("bo0_sb", [P, 1])
        gw_sb = sb("gw_sb", [P, EX])
        gb_sb = sb("gb_sb", [P, EX])
        rms_sb = sb("rms_sb", [P, EX])
        w1_sb = big[:, 46 * S:50 * S].rearrange("p (u c) -> p u c", u=EU)
        b1_sb = sb("b1_sb", [P, EU])
        w2_sb = big[:, 50 * S:54 * S].rearrange("p (u c) -> p u c", u=EU)
        b2_sb = sb("b2_sb", [P, EX])
        b2s = sb("b2s", [P, 1])
        l1w_sb = sb("l1w_sb", [P, 3, D])
        dn_sb = sb("dn_sb", [P, 32])
        up_sb = sb("up_sb", [32, 2, D])
        wo1_sb = sb("wo1_sb", [P, D])
        mw1_sb = sb("mw1_sb", [P, MH])
        mb1_sb = sb("mb1_sb", [P, MU])
        mw2_sb = sb("mw2_sb", [P, MU, D])
        mb2_sb = sb("mb2_sb", [P, 1])
        sc_sb = sb("sc_sb", [P, 1])
        ps = ctx.enter_context(nc.psum_tensor("ps", [P, 8, 512], F32))

        HS = NT * S
        Y = [big[:, n * HS:(n + 1) * HS] for n in range(4)]
        A = [big[:, (4 + n) * HS:(5 + n) * HS] for n in range(2)]
        PT = [big[:, (6 + 4 * n) * HS:(10 + 4 * n) * HS].rearrange("p (j t s) -> p j t s", j=GH, t=NT)
              for n in range(2)]

        class Work:

            def __init__(self, p):
                self.p = p
                self.mb = mbs[:, p, :]
                self.ev = evs[:, p]
                self.tiny = tinies[:, p, :]
                def at(*slots):
                    for n in slots:
                        yield big[:, (23 * p + n) * S:(23 * p + n + 1) * S]

                self.xb, self.xc, self.sq, self.v, self.r, self.t, self.h = at(0, 1, 2, 3, 4, 5, 6)
                self.rest, self.y = at(14, 14)
                self.q, self.k, self.vv, self.den, self.qq, self.kk, self.c, self.nv = at(7, 8, 9, 13, 15, 16, 17, 18)
                self.d = list(at(10, 11, 12))
                self.os, self.oT, self.ao, self.kv, self.lat, self.ngb = at(10, 11, 12, 10, 11, 15)
                self.g = list(at(7, 8, 9, 13))
                self.w1e, self.w2e, self.evm, self.ev2, self.res = at(15, 16, 17, 18, 12)
                pair = lambda n: big[:, (23 * p + n) * S:(23 * p + n) * S + SPLITS * S // 2].bitcast(BF16)\
                    .rearrange("p (a s) -> p a s", a=SPLITS)
                self.pq, self.pk = pair(19), pair(21)

            def bank(self, n):
                return ps[:, 4 * self.p + n, :]

            def sem(self, ph, name):
                return sem(f"{ph}{self.p}_{name}")

        tinies = sb("tinies", [P, PAIR, 32])
        evs = sb("evs", [32, PAIR, 2, P])
        work = [Work(p) for p in range(PAIR)]

        pvs = sb("pvs", [P, 2, S])
        mx = sb("mx", [P, 4, NT])
        nb = sb("nb", [P, 4, NT])
        rec = sb("rec", [P, 2, NT * GH])

        def bank(n):
            return ps[:, n, :]

        block = ctx.enter_context(nc.Block())

        def wait_apart(eng, s, value):
            if not isinstance(value, int):
                value = eng.to_reg(value)
            eng.wait_ge(sem("loaded"), LOADED)
            eng.wait_ge(s, value)

        def in_turns(*steps):
            for _ in zip_longest(*steps):
                pass

        def norm_mean(w):
            nc.tensor.matmul(w.bank(0), mean_w[:, :], w.xb, start=True, stop=True)\
              .then_inc(w.sem("N", "mean"), 1)

        def norm_var(pe, w, n):
            pe.wait_ge(w.sem("N", "sq"), n + 1)
            nc.tensor.matmul(w.bank(1), mean_w[:, :], w.sq, start=True, stop=True)\
              .then_inc(w.sem("N", "var"), 1)

        def norm_pe(pe, w, n):
            pe.wait_ge(w.sem("N", "x"), n + (1 - TURNS))
            norm_mean(w)
            yield
            norm_var(pe, w, n)
            yield

        def norm_act(act, own, w, n):
            act.wait_ge(w.sem("N", "xc"), n + 1)
            nc.scalar.activation(w.sq, w.xc, ACT.Square).then_inc(w.sem("N", "sq"), 1)
            yield
            act.wait_ge(w.sem("N", "v"), n + 1)
            own(nc.scalar.activation(w.r, w.v, ACT.Ln))
            nc.scalar.activation(w.r, w.r, ACT.Exp, scale=-0.5).then_inc(w.sem("N", "r"), 1)
            yield

        def newton(own, v, r, t):
            own(nc.vector.tensor_tensor(t, r, r, ALU.mult))
            own(nc.vector.tensor_tensor(t, t, v, ALU.mult))
            own(nc.vector.tensor_scalar(t, t, -0.5, 1.5, ALU.mult, ALU.add))
            own(nc.vector.tensor_tensor(r, r, t, ALU.mult))

        def norm_dve(dve, own, w, n, shift, gain):
            dve.wait_ge(w.sem("N", "mean"), n + 1)
            nc.vector.tensor_tensor(w.xc, w.xb, w.bank(0), ALU.subtract).then_inc(w.sem("N", "xc"), 1)
            yield
            dve.wait_ge(w.sem("N", "var"), n + 1)
            nc.vector.tensor_scalar(w.v, w.bank(1), LN_EPS, None, ALU.add).then_inc(w.sem("N", "v"), 1)
            yield
            dve.wait_ge(w.sem("N", "r"), n + 1)
            newton(own, w.v, w.r, w.t)
            own(nc.vector.tensor_tensor(w.h, w.xc, w.r, ALU.mult))
            nc.vector.tensor_scalar(w.h, w.h, w.mb[:, gain:gain + 1], w.mb[:, shift:shift + 1],
                                    ALU.mult, ALU.add).then_inc(w.sem("N", "h"), 1)
            yield

        def split(own, w, src, dst, done):
            own(nc.vector.tensor_copy(dst[:, 0, :], src))
            own(nc.vector.tensor_tensor(w.rest, src, dst[:, 0, :], ALU.subtract))
            own(nc.vector.tensor_copy(dst[:, 1, :], w.rest))
            own(nc.vector.tensor_tensor(w.rest, w.rest, dst[:, 1, :], ALU.subtract))
            nc.vector.tensor_copy(dst[:, 2, :], w.rest).then_inc(done, 1)

        def store_parts(sp, ph, layer, w, i, o):
            sp.wait_ge(w.sem(ph, ("pq", "pk")[o]), i + 1 + o)
            for a in range(SPLITS):
                dst = parts[layer, o, bass.ds(i * PAIR + w.p, 1), :, a, :, :].rearrange("o h d t -> (o h) d t")
                sp.dma_start(dst, (w.pq, w.pk)[o][:, a, :]).then_inc(w.sem(ph, "stored"), 16)

        def parts_stored(eng, ph):
            for w in work:
                eng.wait_ge(w.sem(ph, "stored"), 16 + TURNS * 2 * SPLITS * 16)

        def load_x(sp, ph, src, w, i, done):
            wait_apart(sp, done, i + 1)
            sp.dma_start(w.xb, src[:, bass.ts(i * PAIR + w.p, S)]).then_inc(w.sem("N", "load"), 16)

        def values_to_groups(own, w, i, n):
            by = w.bank(n).rearrange("p (t g j d) -> p g t j d", t=NT, g=NG, j=GH)
            for g in range(NG):
                own(nc.vector.tensor_copy(vall[:, bass.ds(i * (PAIR * NG) + (w.p * NG + g), 1), :, :, 0:DH]
                                          .rearrange("p o t j d -> p (o t) j d"), by[:, g]))

        def batch_in_pool(pool, ph, w, i, done, with_out):
            wait_apart(pool, done, i + 1)
            nc.gpsimd.tensor_copy(w.mb, mod[:, bass.ds(i * PAIR + w.p, 1), :].rearrange("p o m -> p (o m)"))\
              .then_inc(w.sem("N", "mb"), 1)
            if with_out:
                for g in range(NG):
                    nc.gpsimd.tensor_copy(
                        w.os.rearrange("p (t g c) -> p t g c", t=NT, g=NG)[:, :, g, :],
                        oall[:, bass.ds(i * (PAIR * NG) + (w.p * NG + g), 1), :, :].rearrange("p o t c -> p (o t) c"))\
                      .then_inc(w.sem(ph, "os"), 1)

        def attn_out_pe(pe, ph, w, i, n, wo):
            pe.wait_ge(w.sem(ph, "os"), i * NG + NG)
            for t in range(NT):
                last = nc.tensor.transpose(w.bank(0)[:, t * P:(t + 1) * P], w.os[:, t * P:(t + 1) * P],
                                           ident[:, :])
            last.then_inc(w.sem("O", "oT"), 1)
            yield
            pe.wait_ge(w.sem("O", "oTs"), n + 1)
            nc.tensor.matmul(w.bank(1), wo[:, :], w.oT, start=True, stop=True)\
              .then_inc(w.sem("O", "ao"), 1)
            yield

        def attn_out_dve(dve, own, ph, w, i, n, bias, gate):
            dve.wait_ge(w.sem("O", "oT"), n + 1)
            nc.vector.tensor_copy(w.oT, w.bank(0)).then_inc(w.sem("O", "oTs"), 1)
            yield
            dve.wait_ge(w.sem("N", "mb"), i + (TURNS * "ACE".index(ph) + 1))
            dve.wait_ge(w.sem("N", "load"), i * 16 + (TURNS * "ACE".index(ph) + 1) * 16)
            dve.wait_ge(w.sem("O", "ao"), n + 1)
            own(nc.vector.tensor_scalar(w.ao, w.bank(1), bias, w.mb[:, gate:gate + 1], ALU.add, ALU.mult))
            nc.vector.tensor_tensor(w.xb, w.xb, w.ao, ALU.add).then_inc(w.sem("N", "x"), 1)
            yield

        def mlp_pe(pe, ph, w, i, n, up, down):
            def rise(u):
                if u >= 2:
                    pe.wait_ge(w.sem(ph, "gelu"), i * n + (u - 1))
                nc.tensor.matmul(w.bank(u % 2), up(u), w.h, start=True, stop=True)\
                  .then_inc(w.sem(ph, "up"), 1)
            rise(0)
            rise(1)
            yield
            for u in range(n):
                if u + 2 < n:
                    rise(u + 2)
                pe.wait_ge(w.sem(ph, "gelu"), i * n + (u + 1))
                nc.tensor.matmul(w.bank(2), down(u), w.g[u % 4], start=(u == 0), stop=(u == n - 1))\
                  .then_inc(w.sem(ph, "down"), 1)
                yield

        def mlp_act(act, ph, w, i, n, bias):
            for u in range(n):
                act.wait_ge(w.sem(ph, "down"), i * n + (u + 1))
                act.wait_ge(w.sem(ph, "up"), i * n + (u + 1))
                nc.scalar.activation(w.g[u % 4], w.bank(u % 2), ACT.Gelu, bias=bias[:, u:u + 1])\
                  .then_inc(w.sem(ph, "gelu"), 1)
                yield

        def each_slot(eng, L, slot, late=0):
            for turn in range(FILL):
                for s in range(UNROLL):
                    slot(s, At(turn, L), lambda n, turn=turn: turn * UNROLL + n >= 0)
            with eng.Fori(FILL, HEADS // UNROLL) as i:
                at = At(i, L)
                for s in range(UNROLL):
                    slot(s, at, lambda n: True)
            end = At(HEADS // UNROLL, L)
            for s in range(LAG[L] + OUT_LAG + late):
                slot(s, end, lambda n: n < 0)

        def attn_sp(sp, L):
            src_of = [parts[LAYER[L], o].rearrange("b (g j) a d t -> (b g) j a d t", g=NG) for o in range(2)]
            with sp.Fori(0, GROUPS // 2) as i:
                for g in range(2):
                    sp.wait_ge(sem("scores"), At(i, L).head * 2 + (8 * g + 1))
                    for a in range(SPLITS):
                        for r in range(SPLITS):
                            row = (a * SPLITS + r) * DH
                            for o, st, part in ((0, qst, r), (1, kst, a)):
                                src = src_of[o][bass.ds(i * 2 + g, 1), :, part, :, :]
                                sp.dma_start(st[row:row + DH, g, :, :], src.rearrange("o j d t -> d (o j) t"))\
                                  .then_inc(sem(f"stack{g}"), 16)

        def attn_pool(pool, L):
            with pool.Fori(0, GROUPS // 2) as i:
                for g in range(2):
                    wait_apart(pool, sem("pv"), At(i, L).group + (g + 1))
                    nc.gpsimd.tensor_copy(
                        vg[:, g, :, :, 0:VC],
                        vall[:, bass.ds(i * 2 + g, 1), :, :, :].rearrange("p o t j c -> p (o t) j c"))\
                      .then_inc(sem("vg"), 1)

        def attn_pe(pe, L, wait_read):
            def scores(n, chunks, at):
                par = (n // GH) % 2
                if n % GH == 0 and chunks[0] == 0:
                    pe.wait_ge(sem(f"stack{par}"), at.turn * STACK + STACK)
                for c in chunks:
                    wait_read(n, c, at)
                    for t in (2 * c, 2 * c + 1):
                        last = nc.tensor.matmul(bank(t), qst[:, par, n % GH, t * P:(t + 1) * P],
                                                kst[:, par, n % GH, :], start=True, stop=True)
                    last.then_inc(sem("scores"), 1)

            def transposes(n, kts, at):
                if kts[0] == 0:
                    pe.wait_ge(sem("probs"), at.head + (n + 1))
                for kt in kts:
                    pe.wait_ge(sem(f"evac{kt % 2}"), at.head * 2 + (2 * n + kt // 2 + 1))
                    for t in range(NT):
                        last = nc.tensor.transpose(ps[:, 4 + kt % 2, t * P:(t + 1) * P],
                                                   Y[n % 4][:, t * S + kt * P:t * S + (kt + 1) * P], ident[:, :])
                    last.then_inc(sem("turned"), 1)

            def values(n, kt, at):
                g, par = n // GH, (n // GH) % 2
                if kt == 0:
                    for k in range(2):
                        pe.wait_ge(sem(f"evac{k}"), at.head * 2 + (8 * g + 9))
                    pe.wait_ge(sem("vg"), at.group + (g + 1))
                    pe.wait_ge(sem("pvs"), at.group + (g + 1))
                for j in range(GH):
                    last = nc.tensor.matmul(ps[32 * j:32 * j + 32, 6, :], vg[:, par, kt, j, :], PT[par][:, j, kt, :],
                                            start=(kt == 0), stop=(kt == NT - 1))
                if kt == NT - 1:
                    last.then_inc(sem("pv"), 1)

            def by_token(n, at):
                g, par = n // GH, (n // GH) % 2
                pe.wait_ge(sem("pvs"), at.group + (g + 2))
                pe.wait_ge(sem("out"), at.group + (g + 1))
                for t in range(NT):
                    last = nc.tensor.transpose(ps[:, 7, t * P:(t + 1) * P], pvs[:, par, t * P:(t + 1) * P],
                                               ident[:, :])
                last.then_inc(sem("pvT"), 1)

            def slot(s, at, on):
                n = s - LAG[L] - 1
                if on(n):
                    transposes(n, (0, 1), at)
                if on(s):
                    scores(s, (0, 1) if L == "B" else (0,), at)
                if on(n):
                    transposes(n, (2, 3), at)
                if n % GH == 1 and on(n - n % GH - 2 * GH):
                    by_token(n - n % GH - 2 * GH, at)
                if on(n - GH):
                    values(n - GH, n % GH, at)
                if on(s) and L == "D":
                    scores(s, (1,), at)
            each_slot(pe, L, slot, 1)

        def group_out_dve(dve, L, n, at, on):
            m = n - n % GH - 2 * GH
            g, par = m // GH, (m // GH) % 2
            if n % GH == 0 and on(m):
                dve.wait_ge(sem("pv"), at.group + (g + 1 + PV0))
                nc.vector.tensor_copy(pvs[:, par, :], bank(6)).then_inc(sem("pvs"), 1)
            if n % GH == 2 and on(m):
                dve.wait_ge(sem("pvT"), at.group + (g + 1))
                by = bank(7).rearrange("p (m c) -> p m c", c=32)
                nc.vector.reciprocal(rec[:, par, :], by[:, :, DH]).then_inc(sem("rec"), 1)
                dve.wait_ge(sem("rec"), at.group + (g + 1))
                dst = oall[:, bass.ds(at.place + g, 1), :, :].rearrange("p o t (j d) -> p (o t j) d", d=DH)
                nc.vector.tensor_tensor(dst, by[:, :, 0:DH],
                                        rec[:, par, :].unsqueeze(2).broadcast_to([P, NT * GH, DH]), ALU.mult)\
                  .then_inc(sem("out"), 1)

        def attn1_act(act):
            def slot(s, at, on):
                if on(s):
                    act.wait_ge(sem("turned"), at.head * 4 + (4 * s + 1))
                    for c in range(2):
                        act.wait_ge(sem("scores"), at.head * 2 + (2 * s + c + 1 + SCORES0))
                        nc.scalar.activation(Y[s % 4][:, c * 2 * S:(c + 1) * 2 * S],
                                             ps[:, 2 * c:2 * c + 2, :].rearrange("p a s -> p (a s)"),
                                             ACT.Square).then_inc(sem("scored"), 1)
                n = s - 1
                if on(n):
                    act.wait_ge(sem("abs"), at.head + (n + 1))
                    nc.scalar.activation(A[n % 2], A[n % 2], ACT.Ln).then_inc(sem("ln"), 1)
                    act.wait_ge(sem("ln"), at.head + (n + 1))
                    nc.scalar.activation(A[n % 2], A[n % 2], ACT.Exp, scale=-2.0).then_inc(sem("inv"), 1)
                n = s - 2
                if on(n):
                    act.wait_ge(sem("bias"), at.head + (n + 1))
                    for t in range(NT):
                        sl = Y[n % 4][:, t * S:(t + 1) * S]
                        last = nc.scalar.activation(sl, sl, ACT.Exp, bias=nb[:, n % 4, t:t + 1], scale=0.5)
                    last.then_inc(sem("probs"), 1)
            each_slot(act, "B", slot)

        def attn1_dve(dve):
            def evac(n, kt, at):
                dve.wait_ge(sem("turned"), at.head * 4 + (4 * n + kt + 1 + TURNED0))
                nc.vector.tensor_copy(PT[(n // GH) % 2][:, n % GH, kt, :], bank(4 + kt % 2))\
                  .then_inc(sem(f"evac{kt % 2}"), 1)

            def slot(s, at, on):
                if on(s):
                    dve.wait_ge(sem("scored"), at.head * 2 + (2 * s + 4))
                    nc.vector.tensor_scalar(Y[s % 4], Y[s % 4], 1.0, ZERO_GUARD, ALU.subtract, ALU.subtract)\
                      .then_inc(sem("den"), 1)
                    dve.wait_ge(sem("den"), at.head + (s + 1))
                    nc.vector.tensor_scalar(A[s % 2].bitcast(U32), Y[s % 4].bitcast(U32), 0x7fffffff, None,
                                            ALU.bitwise_and).then_inc(sem("abs"), 1)
                n, m = s - 1, s - 3
                group_out_dve(dve, "B", m, at, on)
                if on(m):
                    evac(m, 0, at)
                    evac(m, 1, at)
                for t in range(NT):
                    if on(n):
                        if t == 0:
                            wait_apart(dve, sem("inv"), at.head + (n + 1))
                        sl = slice(t * S, (t + 1) * S)
                        nc.vector.tensor_tensor_reduce(out=Y[n % 4][:, sl], in0=Y[n % 4][:, sl], in1=A[n % 2][:, sl],
                                                       scale=-1.0, scalar=-3e38, op0=ALU.mult, op1=ALU.max,
                                                       accum_out=mx[:, n % 4, t:t + 1]).then_inc(sem("quot"), 1)
                    if on(m) and t in (1, 2):
                        evac(m, t + 1, at)
                if on(n):
                    dve.wait_ge(sem("quot"), at.head * 4 + (4 * n + 4 + QUOT0))
                    nc.vector.tensor_scalar(nb[:, n % 4, :], mx[:, n % 4, :], -0.5, None, ALU.mult)\
                      .then_inc(sem("bias"), 1)
            each_slot(dve, "B", slot)

        def attn2_act(act):
            def slot(s, at, on):
                for t in range(NT):
                    n = s - 1
                    if on(n):
                        if t == 0:
                            act.wait_ge(sem("bias"), at.head + (n + 1))
                        sl = Y[n % 4][:, t * S:(t + 1) * S]
                        ins = nc.scalar.activation(sl, sl, ACT.Exp, bias=nb[:, n % 4, t:t + 1], scale=DOT_SCALE)
                        if t == NT - 1:
                            ins.then_inc(sem("probs"), 1)
                    n = s - 2
                    if on(n) and t % 2:
                        act.wait_ge(sem("turned"), at.head * 4 + (4 * n + t + 1 + TURNED0))
                        nc.scalar.activation(PT[(n // GH) % 2][:, n % GH, t, :], bank(5), ACT.Copy)\
                          .then_inc(sem("evac1"), 1)
            each_slot(act, "D", slot)

        def attn2_dve(dve):
            def slot(s, at, on):
                for t in range(NT):
                    if on(s):
                        if t == 0:
                            dve.wait_ge(sem("turned"), at.head * 4 + (4 * s + 1))
                        wait_apart(dve, sem("scores"), at.head * 2 + (2 * s + t // 2 + 1 + SCORES0))
                        nc.vector.tensor_tensor_reduce(out=Y[s % 4][:, t * S:(t + 1) * S], in0=bank(t),
                                                       in1=decay[:, t, :],
                                                       scale=1.0, scalar=-3e38, op0=ALU.mult, op1=ALU.max,
                                                       accum_out=mx[:, s % 4, t:t + 1]).then_inc(sem("quot"), 1)
                    n = s - 2
                    if on(n) and t % 2:
                        dve.wait_ge(sem("turned"), at.head * 4 + (4 * n + t + TURNED0))
                        nc.vector.tensor_copy(PT[(n // GH) % 2][:, n % GH, t - 1, :], bank(4)).then_inc(sem("evac0"), 1)
                if on(s):
                    dve.wait_ge(sem("quot"), at.head * 4 + (4 * s + 4 + QUOT0))
                    nc.vector.tensor_scalar(nb[:, s % 4, :], mx[:, s % 4, :], -DOT_SCALE, None, ALU.mult)\
                      .then_inc(sem("bias"), 1)
                group_out_dve(dve, "D", s - 2, at, on)
            each_slot(dve, "D", slot)

        loads = [(c_sb[:, :, :], cT), (wmod_sb[:, :, :], wmod), (mean_w[:, :], blk_in[:, 0, :]),
                 (ident[:, :], ident_in), (blk[:, :], blk_in[:, 1, :]), (ones[:, :], blk_in[:, 2, :]),
                 (w_qkv[:, :, :], wqkv), (b_qkv[:, :], bqkv), (al[:, :], alpha.partition_broadcast(P)),
                 (decay[:, :, :], decay_in), (wo0_sb[:, :], wo0), (bo0_sb[:, :], bo0), (gw_sb[:, :], gwT),
                 (gb_sb[:, :], gb.partition_broadcast(P)), (rms_sb[:, :], rms.partition_broadcast(P)),
                 (b1_sb[:, :], b1), (b2_sb[:, :], b2),
                 (l1w_sb[:, :, :], l1w), (dn_sb[:, :], l1down), (up_sb[:, :, :], l1up), (wo1_sb[:, :], l1wo),
                 (mw1_sb[:, :], mw1), (mb1_sb[:, :], mb1), (mw2_sb[:, :, :], mw2), (mb2_sb[:, :], mb2),
                 (sc_sb[:, :], scale.partition_broadcast(P))]
        LOADED = 16 * len(loads)

        @block.sync
        def _(sp):
            for dst, src in loads:
                sp.dma_start(dst, src).then_inc(sem("loaded"), 16)
            sp.wait_ge(sem("modps"), 1)
            with sp.Fori(0, TURNS) as i:
                for w in work:
                    load_x(sp, "A", xT, w, i, w.sem("A", "pk"))
                for o in range(2):
                    for w in work:
                        store_parts(sp, "A", 0, w, i, o)
            parts_stored(sp, "A")
            sp.wait_ge(sem("zeros"), 4)
            attn_sp(sp, "B")
            sp.wait_ge(sem("out"), GROUPS + 1)
            sp.dma_start(w1_sb, w1).then_inc(sem("experts"), 16)
            sp.dma_start(w2_sb, w2).then_inc(sem("experts"), 16)
            with sp.Fori(0, TURNS) as i:
                for w in work:
                    wait_apart(sp, w.sem("C", "xst"), i * 16 + 16)
                    load_x(sp, "C", xT, w, i, w.sem("C", "pk"))
                for w in work:
                    sp.wait_ge(w.sem("N", "x"), i * 2 + 2)
                    sp.dma_start(x1[:, bass.ts(i * PAIR + w.p, S)], w.xb).then_inc(w.sem("C", "xst"), 16)
                for o in range(2):
                    for w in work:
                        store_parts(sp, "C", 1, w, i, o)
            parts_stored(sp, "C")
            for w in work:
                sp.wait_ge(w.sem("C", "xst"), 16 + 16 * TURNS)
            attn_sp(sp, "D")
            sp.wait_ge(sem("out"), 2 * GROUPS + 1)
            with sp.Fori(0, TURNS) as i:
                for w in work:
                    load_x(sp, "E", x1, w, i, w.sem("E", "res"))
                for w in work:
                    sp.wait_ge(w.sem("E", "res"), i + 2)
                    sp.dma_start(out[:, bass.ts(i * PAIR + w.p, S)], w.res).then_inc(w.sem("E", "outd"), 16)
            for w in work:
                sp.wait_ge(w.sem("E", "outd"), 16 + 16 * TURNS)

        @block.gpsimd
        def _(pool):
            first = [("scored", 2), ("quot", QUOT0), ("turned", TURNED0), ("scores", SCORES0), ("pv", PV0),
                     ("pvs", 1), ("out", 1), ("evac0", 1), ("evac1", 1)]
            for p in range(PAIR):
                first += [(f"A{p}_pk", 1), (f"C{p}_pk", 1), (f"E{p}_res", 1), (f"A{p}_stored", 16),
                          (f"C{p}_stored", 16), (f"C{p}_xst", 16), (f"E{p}_outd", 16),
                          (f"C{p}_down", DOWN0), (f"E{p}_down", DOWN0)]
            for n, (name, count) in enumerate(first):
                nc.gpsimd.memset(small[:, n:n + 1], 0.0).then_inc(sem(name), count)
            nc.gpsimd.memset(s_base[:, :], YAT_BASE).then_inc(sem("base"), 1)
            nc.gpsimd.memset(vg[:, :, :, :, :], 0.0).then_inc(sem("zeros"), 1)
            nc.gpsimd.memset(vall[:, :, :, :, DH:VC], 1.0).then_inc(sem("zeros"), 1)
            pool.wait_ge(sem("loaded"), LOADED)
            pool.wait_ge(sem("base"), 1)
            nc.gpsimd.tensor_tensor(s_yat[:, :], s_base[:, :], al[:, :], ALU.pow).then_inc(sem("yat"), 1)
            pool.wait_ge(sem("mod"), 1)
            with pool.Fori(0, TURNS) as i:
                for w in work:
                    batch_in_pool(pool, "A", w, i, w.sem("A", "pk"), False)
            for w in work:
                pool.wait_ge(w.sem("A", "pk"), TURNS + 1)
            pool.wait_ge(sem("zeros"), 4)
            attn_pool(pool, "B")
            pool.wait_ge(sem("out"), GROUPS + 1)
            with pool.Fori(0, TURNS) as i:
                for w in work:
                    batch_in_pool(pool, "C", w, i, w.sem("C", "pk"), True)
            for w in work:
                pool.wait_ge(w.sem("C", "pk"), TURNS + 1)
            attn_pool(pool, "D")
            pool.wait_ge(sem("out"), 2 * GROUPS + 1)
            with pool.Fori(0, TURNS) as i:
                for w in work:
                    batch_in_pool(pool, "E", w, i, w.sem("E", "res"), True)

        def first_guess(act, own, ready, v, r, done, i):
            act.wait_ge(ready, i + 1)
            own(nc.scalar.activation(r, v, ACT.Ln))
            nc.scalar.activation(r, r, ACT.Exp, scale=-0.5).then_inc(done, 1)

        def a_act(act, w, i):
            own = Order(act, w.sem("N", "act"), own_base("act", "A", i))
            yield from norm_act(act, own, w, i)
            act.wait_ge(w.sem("N", "h"), i + 1)
            nc.scalar.activation(w.sq, w.h, ACT.Square).then_inc(w.sem("A", "h2"), 1)
            act.wait_ge(w.sem("A", "dot"), i + 1)
            for j in range(3):
                nc.scalar.activation(w.d[j], w.bank(1 + j), ACT.Square).then_inc(w.sem("A", "d2"), 1)
            yield
            act.wait_ge(w.sem("A", "qkv"), i * 3 + 1)
            nc.scalar.activation(w.qq, w.q, ACT.Square).then_inc(w.sem("A", "qq"), 1)
            act.wait_ge(w.sem("A", "qkv"), i * 3 + 2)
            nc.scalar.activation(w.kk, w.k, ACT.Square).then_inc(w.sem("A", "qq"), 1)
            yield
            first_guess(act, own, w.sem("A", "nv"), w.nv, w.c, w.sem("A", "c"), i)
            assert own.n == OWN["actA"]

        def c_act(act, w, i):
            own = Order(act, w.sem("N", "act"), own_base("act", "C", i))
            yield from norm_act(act, own, w, i * 2 + TURNS)
            first_guess(act, own, w.sem("C", "ms"), w.tiny[:, 0:4], w.tiny[:, 4:8], w.sem("C", "rms"), i)
            yield
            act.wait_ge(w.sem("C", "lm"), i + 1)
            nc.scalar.activation(w.t[:, 32:64], w.t[:, 0:32], ACT.Exp, scale=2.0).then_inc(w.sem("C", "le"), 1)
            yield
            yield from mlp_act(act, "C", w, i, EU, b1_sb)
            yield from norm_act(act, own, w, i * 2 + (TURNS + 1))
            assert own.n == OWN["actC"]

        def e_act(act, w, i):
            own = Order(act, w.sem("N", "act"), own_base("act", "E", i))
            yield from norm_act(act, own, w, i + 3 * TURNS)
            yield from mlp_act(act, "E", w, i, MU, mb1_sb)
            assert own.n == OWN["actE"]

        @block.scalar
        def _(act):
            act.wait_ge(sem("loaded"), LOADED)
            nc.scalar.preload_act_table_set("natural_log_exp_and_others")
            nc.scalar.activation(sil[:, 0], c_sb[:, :, :], ACT.Exp, scale=-1.0).then_inc(sem("sil_e"), 1)
            with act.Fori(0, TURNS) as i:
                in_turns(*(a_act(act, w, i) for w in work))
            attn1_act(act)
            with act.Fori(0, TURNS) as i:
                nc.scalar.preload_act_table_set("natural_log_exp_and_others")
                in_turns(*(c_act(act, w, i) for w in work))
            nc.scalar.preload_act_table_set("natural_log_exp_and_others")
            attn2_act(act)
            with act.Fori(0, TURNS) as i:
                nc.scalar.preload_act_table_set("natural_log_exp_and_others")
                in_turns(*(e_act(act, w, i) for w in work))

        def a_pe(pe, w, i):
            pe.wait_ge(w.sem("N", "load"), i * 16 + 16)
            norm_mean(w)
            yield
            norm_var(pe, w, i)
            yield
            pe.wait_ge(w.sem("N", "h"), i + 1)
            for j in range(3):
                last = nc.tensor.matmul(w.bank(1 + j), w_qkv[:, j, :], w.h, start=True, stop=True)
            last.then_inc(w.sem("A", "dot"), 1)
            pe.wait_ge(w.sem("A", "h2"), i + 1)
            nc.tensor.matmul(w.bank(0), ones[:, :], w.sq, start=True, stop=True).then_inc(w.sem("A", "n2"), 1)
            yield
            pe.wait_ge(w.sem("A", "s2"), i + 1)
            nc.tensor.matmul(w.bank(0), blk[:, :], w.qq, start=True, stop=True).then_inc(w.sem("A", "nn"), 1)
            pe.wait_ge(w.sem("A", "qkv"), i * 3 + 3)
            for t in range(NT):
                last = nc.tensor.transpose(w.bank(1)[:, t * P:(t + 1) * P], w.vv[:, t * P:(t + 1) * P], ident[:, :])
            last.then_inc(w.sem("A", "vt"), 1)

        def c_pe(pe, w, i):
            yield from attn_out_pe(pe, "C", w, i, i, wo0_sb)
            yield from norm_pe(pe, w, i * 2 + TURNS)
            pe.wait_ge(w.sem("N", "h"), i * 2 + (TURNS + 1))
            for t in range(NT):
                last = nc.tensor.matmul(w.bank(2)[:, t * EX:(t + 1) * EX], w.h[:, t * P:(t + 1) * P], gw_sb[:, :],
                                        start=True, stop=True)
            last.then_inc(w.sem("C", "lg"), 1)
            yield
            pe.wait_ge(w.sem("C", "ng"), i + 1)
            for t in range(NT):
                last = nc.tensor.matmul(w.bank(3)[:, t * P:(t + 1) * P],
                                        w.tiny[:, 12 + t:13 + t].broadcast_to([P, P]), ident[:, :],
                                        start=True, stop=True)
            last.then_inc(w.sem("C", "ngb"), 1)
            yield
            pe.wait_ge(sem("experts"), 32)
            yield from mlp_pe(pe, "C", w, i, EU, lambda u: w1_sb[:, u, :], lambda u: w2_sb[:, u, :])
            yield from norm_pe(pe, w, i * 2 + (TURNS + 1))
            pe.wait_ge(w.sem("N", "h"), i * 2 + (TURNS + 2))
            nc.tensor.matmul(w.bank(3), l1w_sb[:, 1, :], w.h, start=True, stop=False)
            nc.tensor.matmul(w.bank(3), l1w_sb[:, 2, :], w.h, start=False, stop=True).then_inc(w.sem("C", "kv"), 1)
            nc.tensor.matmul(w.bank(2), l1w_sb[:, 0, :], w.h, start=True, stop=True).then_inc(w.sem("C", "qp"), 1)
            yield
            pe.wait_ge(w.sem("C", "kvs"), i + 1)
            nc.tensor.matmul(w.bank(0)[0:32, :], dn_sb[:, :], w.kv, start=True, stop=True).then_inc(w.sem("C", "lat"), 1)
            yield
            pe.wait_ge(w.sem("C", "lats"), i + 1)
            nc.tensor.matmul(w.bank(1), up_sb[:, 0, :], w.lat[0:32, :], start=True, stop=True)
            for t in range(NT):
                last = nc.tensor.matmul(w.bank(3)[:, t * P:(t + 1) * P], w.lat[0:32, t * P:(t + 1) * P],
                                        up_sb[:, 1, :], start=True, stop=True)
            last.then_inc(w.sem("C", "rec"), 1)

        def e_pe(pe, w, i):
            yield from attn_out_pe(pe, "E", w, i, i + TURNS, wo1_sb)
            yield from norm_pe(pe, w, i + 3 * TURNS)
            pe.wait_ge(w.sem("N", "h"), i + (3 * TURNS + 1))
            for k in range(2):
                last = nc.tensor.transpose(w.bank(2)[0:32, k * P:(k + 1) * P], w.h[:, 1 + k:33 + k], ident[:, :])
            last.then_inc(w.sem("E", "rows"), 1)
            yield
            pe.wait_ge(w.sem("E", "ev"), i + 1)
            nc.tensor.matmul(w.bank(3), w.ev[:, 1, :], w.evm[0:32, :], start=True, stop=True)
            for t in range(MU):
                last = nc.tensor.matmul(w.bank(2)[:, t * P:(t + 1) * P], w.ev[:, 1, :],
                                        w.ev2[0:32, t * P:(t + 1) * P], start=True, stop=True)
            last.then_inc(w.sem("E", "delta"), 1)
            yield
            pe.wait_ge(w.sem("E", "weights"), i + 1)
            yield from mlp_pe(pe, "E", w, i, MU, lambda u: w.w1e[:, u * P:(u + 1) * P],
                              lambda u: w.w2e[:, u * P:(u + 1) * P])

        @block.tensor
        def _(pe):
            pe.wait_ge(sem("sil"), 1)
            for l in range(2):
                for m in range(6):
                    last = nc.tensor.matmul(ps[:, 0, (6 * l + m) * B:(6 * l + m + 1) * B],
                                            wmod_sb[:, l, m * D:(m + 1) * D], sil[:, 3, l, :], start=True, stop=True)
            last.then_inc(sem("modps"), 1)
            pe.wait_ge(sem("wsq"), 1)
            for j in range(3):
                last = nc.tensor.matmul(ps[:, 4, j:j + 1], work[0].d[0][:, j * D:(j + 1) * D], ones[:, 0:1],
                                        start=True, stop=True)
            last.then_inc(sem("wn"), 1)
            pe.wait_ge(sem("wns"), 1)
            with pe.Fori(0, TURNS) as i:
                in_turns(*(a_pe(pe, w, i) for w in work))
            pe.wait_ge(sem("zeros"), 4)
            attn_pe(pe, "B", lambda n, c, at: pe.wait_ge(sem("scored"), at.head * 2 + (2 * n + c + 1)))
            with pe.Fori(0, TURNS) as i:
                in_turns(*(c_pe(pe, w, i) for w in work))
            attn_pe(pe, "D", lambda n, c, at: pe.wait_ge(sem("quot"), at.head * 4 + (4 * n + 2 * c + 1)))
            with pe.Fori(0, TURNS) as i:
                in_turns(*(e_pe(pe, w, i) for w in work))

        def a_dve(dve, w, i):
            own = Order(dve, w.sem("N", "dve"), own_base("dve", "A", i))
            dve.wait_ge(w.sem("N", "mb"), i + 1)
            dve.wait_ge(w.sem("N", "load"), i * 16 + 16)
            yield from norm_dve(dve, own, w, i, SA, CA)
            dve.wait_ge(w.sem("A", "n2"), i + 1)
            dve.wait_ge(w.sem("A", "d2"), i * 3 + 3)
            for j, dst in enumerate((w.q, w.k, w.vv)):
                own(nc.vector.tensor_scalar(w.den, w.bank(0), wn[:, j:j + 1], None, ALU.add))
                own(nc.vector.scalar_tensor_tensor(w.y, w.bank(1 + j), -2.0, w.den, ALU.mult, ALU.add))
                own(nc.vector.reciprocal(w.den, w.y))
                own(nc.vector.tensor_tensor(w.y, w.d[j], w.den, ALU.mult))
                nc.vector.tensor_scalar(dst, w.y, b_qkv[:, j:j + 1], s_yat[:, j:j + 1],
                                        ALU.add, ALU.mult).then_inc(w.sem("A", "qkv"), 1)
            dve.wait_ge(w.sem("A", "qq"), i * 2 + 2)
            nc.vector.tensor_tensor(w.qq, w.qq, w.kk, ALU.add).then_inc(w.sem("A", "s2"), 1)
            yield
            dve.wait_ge(w.sem("A", "nn"), i + 1)
            nc.vector.tensor_scalar(w.nv, w.bank(0), ATT_EPS, 0.5, ALU.add, ALU.mult)\
              .then_inc(w.sem("A", "nv"), 1)
            dve.wait_ge(w.sem("A", "vt"), i + 1)
            values_to_groups(own, w, i, 1)
            yield
            dve.wait_ge(w.sem("A", "c"), i + 1)
            newton(own, w.nv, w.c, w.t)
            own(nc.vector.tensor_tensor(w.q, w.q, w.c, ALU.mult))
            dve.wait_ge(w.sem("A", "stored"), i * (2 * SPLITS * 16) + 16)
            split(own, w, w.q, w.pq, w.sem("A", "pq"))
            dve.wait_ge(w.sem("A", "pq"), i + 1)
            split(own, w, w.k, w.pk, w.sem("A", "pk"))
            assert own.n == OWN["dveA"]

        def c_dve(dve, w, i):
            own = Order(dve, w.sem("N", "dve"), own_base("dve", "C", i))
            yield from attn_out_dve(dve, own, "C", w, i, i, bo0_sb[:, 0:1], GA)
            yield from norm_dve(dve, own, w, i * 2 + TURNS, SB, CB)
            lg = w.t[:, 0:32].rearrange("p (t e) -> p t e", e=EX)
            l2 = w.t[:, 32:64].rearrange("p (t e) -> p t e", e=EX)
            tiny = w.tiny
            by_expert = lambda v: v[:, :].unsqueeze(1).broadcast_to([P, NT, EX])
            by_token = lambda c: tiny[:, c:c + NT].unsqueeze(2).broadcast_to([P, NT, EX])
            dve.wait_ge(w.sem("C", "lg"), i + 1)
            own(nc.vector.tensor_tensor(lg, w.bank(2)[:, 0:32].rearrange("p (t e) -> p t e", e=EX),
                                        by_expert(gb_sb), ALU.add))
            own(nc.vector.tensor_tensor(l2, lg, lg, ALU.mult))
            own(nc.vector.reduce_sum(tiny[:, 8:12], l2, axis=AX_X))
            nc.vector.tensor_scalar(tiny[:, 0:4], tiny[:, 8:12], 1 / EX, RMS_EPS, ALU.mult, ALU.add)\
              .then_inc(w.sem("C", "ms"), 1)
            yield
            dve.wait_ge(w.sem("C", "rms"), i + 1)
            newton(own, tiny[:, 0:4], tiny[:, 4:8], tiny[:, 16:20])
            own(nc.vector.tensor_tensor(lg, lg, by_token(4), ALU.mult))
            own(nc.vector.tensor_tensor(lg, lg, by_expert(rms_sb), ALU.mult))
            own(nc.vector.reduce_max(tiny[:, 8:12], lg, axis=AX_X))
            nc.vector.tensor_tensor(lg, lg, by_token(8), ALU.subtract).then_inc(w.sem("C", "lm"), 1)
            yield
            dve.wait_ge(w.sem("C", "le"), i + 1)
            own(nc.vector.reduce_sum(tiny[:, 16:20], l2, axis=AX_X))
            own(nc.vector.tensor_scalar(tiny[:, 16:20], tiny[:, 16:20], NORM_EPS, 1.0, ALU.mult, ALU.add))
            nc.vector.reciprocal(tiny[:, 12:16], tiny[:, 16:20]).then_inc(w.sem("C", "ng"), 1)
            yield
            dve.wait_ge(w.sem("C", "ngb"), i + 1)
            own(nc.vector.tensor_copy(w.ngb, w.bank(3)))
            yield
            dve.wait_ge(w.sem("C", "down"), i * EU + (EU + DOWN0))
            own(nc.vector.tensor_scalar(w.y, w.bank(2), b2s[:, 0:1], None, ALU.add))
            own(nc.vector.tensor_tensor(w.y, w.y, w.ngb, ALU.mult))
            nc.vector.scalar_tensor_tensor(w.xb, w.y, w.mb[:, GB:GB + 1], w.xb, ALU.mult, ALU.add)\
              .then_inc(w.sem("N", "x"), 1)
            yield
            yield from norm_dve(dve, own, w, i * 2 + (TURNS + 1), 6 + SA, 6 + CA)
            dve.wait_ge(w.sem("C", "kv"), i + 1)
            nc.vector.tensor_copy(w.kv, w.bank(3)).then_inc(w.sem("C", "kvs"), 1)
            yield
            dve.wait_ge(w.sem("C", "lat"), i + 1)
            nc.vector.tensor_copy(w.lat[0:32, :], w.bank(0)[0:32, :]).then_inc(w.sem("C", "lats"), 1)
            dve.wait_ge(w.sem("C", "qp"), i + 1)
            dve.wait_ge(w.sem("C", "stored"), i * (2 * SPLITS * 16) + 16)
            split(own, w, w.bank(2), w.pq, w.sem("C", "pq"))
            dve.wait_ge(w.sem("C", "pq"), i + 1)
            yield
            dve.wait_ge(w.sem("C", "rec"), i + 1)
            values_to_groups(own, w, i, 3)
            split(own, w, w.bank(1), w.pk, w.sem("C", "pk"))
            assert own.n == OWN["dveC"]

        def e_dve(dve, w, i):
            own = Order(dve, w.sem("N", "dve"), own_base("dve", "E", i))
            yield from attn_out_dve(dve, own, "E", w, i, i + TURNS, 0.0, 6 + GA)
            yield from norm_dve(dve, own, w, i + 3 * TURNS, 6 + SB, 6 + CB)
            dve.wait_ge(w.sem("E", "rows"), i + 1)
            own(nc.vector.tensor_copy(w.ev, w.bank(2)[0:32, 0:2 * P].rearrange("p (k c) -> p k c", k=2)))
            for m in range(MU):
                own(nc.vector.tensor_scalar(w.evm[0:32, m * P:(m + 1) * P], w.ev[:, 0, :],
                                            ident[0:32, 2 * m:2 * m + 1], None, ALU.mult))
            turned = w.ev[:, 0, :].rearrange("p (r t) -> p t r", t=MU)
            for m in range(MU):
                dst = w.ev2[0:32, :].rearrange("p (t i r) -> p t i r", t=MU, i=MU)[:, :, m, :]
                ins = nc.vector.tensor_scalar(dst, turned, ident[0:32, 2 * MU + 2 * m:2 * MU + 2 * m + 1],
                                              None, ALU.mult)
                if m < MU - 1:
                    own(ins)
                else:
                    ins.then_inc(w.sem("E", "ev"), 1)
            yield
            dve.wait_ge(w.sem("E", "delta"), i + 1)
            own(nc.vector.scalar_tensor_tensor(w.w1e, w.bank(3), sc_sb[:, 0:1], mw1_sb[:, :], ALU.mult, ALU.add))
            nc.vector.scalar_tensor_tensor(w.w2e, w.bank(2), sc_sb[:, 0:1],
                                           mw2_sb[:, :, :].rearrange("p u d -> p (u d)"), ALU.mult, ALU.add)\
              .then_inc(w.sem("E", "weights"), 1)
            yield
            dve.wait_ge(w.sem("E", "down"), i * MU + (MU + DOWN0))
            own(nc.vector.tensor_scalar(w.y, w.bank(2), mb2_sb[:, 0:1], w.mb[:, 6 + GB:7 + GB], ALU.add, ALU.mult))
            dve.wait_ge(w.sem("E", "outd"), i * 16 + 16)
            nc.vector.tensor_tensor(w.res, w.y, w.xb, ALU.add).then_inc(w.sem("E", "res"), 1)
            assert own.n == OWN["dveE"]

        @block.vector
        def _(dve):
            nc.vector.memset(qst[:, :, :, :], 0.0).then_inc(sem("zeros"), 1)
            nc.vector.memset(kst[:, :, :, :], 0.0).then_inc(sem("zeros"), 1)
            dve.wait_ge(sem("loaded"), LOADED)
            own = Order(dve, sem("P_dve"), 0)
            dve.wait_ge(sem("sil_e"), 1)
            own(nc.vector.tensor_scalar(sil[:, 1], sil[:, 0], 1.0, None, ALU.add))
            own(nc.vector.reciprocal(sil[:, 2], sil[:, 1]))
            nc.vector.tensor_tensor(sil[:, 3], c_sb[:, :, :], sil[:, 2], ALU.mult).then_inc(sem("sil"), 1)
            nc.vector.tensor_tensor(work[0].d[0][:, 0:3 * D].rearrange("p (j d) -> p j d", j=3), w_qkv[:, :, :],
                                    w_qkv[:, :, :], ALU.mult).then_inc(sem("wsq"), 1)
            dve.wait_ge(sem("modps"), 1)
            own(nc.vector.tensor_copy(mod[:, :, :].rearrange("p b m -> p m b"),
                                      ps[:, 0, 0:12 * B].rearrange("p (m b) -> p m b", b=B)))
            for m in (CA, CB, 6 + CA, 6 + CB):
                own(nc.vector.tensor_scalar(mod[:, :, m], mod[:, :, m], 1.0, None, ALU.add))
            for m in (GA, GB, 6 + GA, 6 + GB):
                g, size, sign = mod[:, :, m], tinies[:, 0, 0:B], tinies[:, 0, B:2 * B]
                own(nc.vector.tensor_scalar(size, g, -1.0, 0.25, ALU.mult, ALU.max))
                own(nc.vector.tensor_tensor(size, size, g, ALU.max))
                own(nc.vector.tensor_scalar(sign, g, 0.0, 2.0, ALU.is_ge, ALU.mult))
                own(nc.vector.tensor_scalar(sign, sign, -1.0, None, ALU.add))
                own(nc.vector.tensor_tensor(g, size, sign, ALU.mult))
            nc.vector.reduce_sum(b2s[:, :], b2_sb[:, :], axis=AX_X).then_inc(sem("mod"), 1)
            dve.wait_ge(sem("wn"), 1)
            nc.vector.tensor_scalar(wn[:, :], ps[:, 4, 0:3], ATT_EPS, None, ALU.add).then_inc(sem("wns"), 1)
            dve.wait_ge(sem("mod"), 1)
            dve.wait_ge(sem("wns"), 1)
            dve.wait_ge(sem("yat"), 1)

            with dve.Fori(0, TURNS) as i:
                in_turns(*(a_dve(dve, w, i) for w in work))
            attn1_dve(dve)
            with dve.Fori(0, TURNS) as i:
                in_turns(*(c_dve(dve, w, i) for w in work))
            attn2_dve(dve)
            with dve.Fori(0, TURNS) as i:
                in_turns(*(e_dve(dve, w, i) for w in work))


def kernel(**inputs):
    import concourse.bacc as bacc
    from concourse.bass_utils import run_bass_kernel_spmd

    a = {k: np.asarray(v) for k, v in inputs.items()}
    col = lambda v: np.ascontiguousarray(v.reshape(-1, 1))
    d = np.arange(D)
    i = np.arange(S, dtype=np.float32)
    decay = np.exp(-np.float32(0.01) * np.abs(i[:, None] - i[None, :])).astype(np.float32)
    consts = np.stack([np.full((D, D), 1 / D), d[:, None] // DH == d[None, :] // DH, np.ones((D, D))],
                      axis=1).astype(np.float32)
    lay = {
        "xT": a["L0_attn_inputs_q"].reshape(B * S, D).T,
        "cT": np.stack([a["L0_c"].T, a["L1_c"].T], axis=1),
        "wmod": np.stack([a["L0_wmod"], a["L1_wmod"]], axis=1),
        "wqkv": np.stack([a["L0_attn_wq"], a["L0_attn_wk"], a["L0_attn_wv"]], axis=1),
        "bqkv": np.stack([a["L0_attn_bq"], a["L0_attn_bk"], a["L0_attn_bv"]], axis=1),
        "alpha": np.concatenate([a["L0_attn_aq"], a["L0_attn_ak"], a["L0_attn_av"]]),
        "wo0": a["L0_attn_wo"], "bo0": col(a["L0_attn_bo"]),
        "gwT": a["L0_ffn_gate_w"].T, "gb": a["L0_ffn_gate_b"], "rms": a["L0_ffn_rms_w"],
        "w1": a["L0_ffn_w1"].transpose(1, 0, 2).reshape(D, EU, P),
        "b1": a["L0_ffn_b1"].reshape(EU, P).T,
        "w2": a["L0_ffn_w2"].reshape(EU, P, D).transpose(1, 0, 2),
        "b2": a["L0_ffn_b2"].T,
        "l1w": np.stack([a["L1_attn_W_q"], a["L1_attn_W_k"], a["L1_attn_W_v"]], axis=1),
        "l1down": a["L1_attn_W_down_kv"],
        "l1up": np.stack([a["L1_attn_W_up_k"], a["L1_attn_W_up_v"]], axis=1),
        "l1wo": a["L1_attn_W_o"],
        "mw1": a["L1_ffn_W1"].T, "mb1": a["L1_ffn_b1"].reshape(MU, P).T,
        "mw2": a["L1_ffn_W2"].T.reshape(MU, P, D).transpose(1, 0, 2), "mb2": col(a["L1_ffn_b2"]),
        "scale": a["L1_ffn_scale"].reshape(1),
        "ident_in": np.eye(P, dtype=np.float32),
        "blk_in": consts,
        "decay_in": decay.reshape(NT, P, S).transpose(1, 0, 2),
    }
    nc = bacc.Bacc("TRN2", target_bir_lowering=False, num_devices=1)
    arrays, args = {}, {}
    for name, v in lay.items():
        arrays[f"in_{name}"] = np.ascontiguousarray(v)
        args[name] = nc.dram_tensor(f"in_{name}", v.shape, mybir.dt.from_np(v.dtype), kind="ExternalInput").ap()
    x1 = nc.dram_tensor("x1", (D, B * S), F32, kind="Internal").ap()
    parts = nc.dram_tensor("parts", (2, 2, B, H, SPLITS, DH, S), BF16, kind="Internal").ap()
    out = nc.dram_tensor("out_0", (D, B * S), F32, kind="ExternalOutput").ap()
    build(nc, parts=parts, x1=x1, out=out, **args)
    r = run_bass_kernel_spmd(nc, [arrays], core_ids=[0])
    return np.ascontiguousarray(r.results[0]["out_0"].T).reshape(B, S, D)
```

```python
import math
from itertools import zip_longest
from contextlib import ExitStack

import numpy as np
import concourse.bass as bass
from concourse import mybir

F32 = mybir.dt.float32
BF16 = mybir.dt.bfloat16
U32 = mybir.dt.uint32
ALU = mybir.AluOpType
ACT = mybir.ActivationFunctionType
AX_X = mybir.AxisListType.X

B, S, D = 8, 512, 128
H, DH = 16, 8
P = 128
NT = S // P
GH = 4
NG = H // GH
GROUPS = B * NG
HEADS = B * H
SPLITS = 3
KROWS = SPLITS * SPLITS * DH
VC = DH + 1
EX, HID = 8, 256
EU = EX * HID // P
MH = 512
MU = MH // P
LN_EPS = 1e-5
ATT_EPS = 1e-5
RMS_EPS = float(np.finfo(np.float32).eps)
NORM_EPS = 1e-6
YAT_BASE = math.sqrt(D) / math.log(1 + D)
DOT_SCALE = 1 / math.sqrt(D)
ZERO_GUARD = 1e-12
SA, CA, GA, SB, CB, GB = range(6)
LAYER = {"B": 0, "D": 1}
LAG = {"B": 3, "D": 2}
UNROLL = 8
OUT_LAG = 7
FILL = 2
PAIR = 2
TURNS = B // PAIR


class Order:

    def __init__(self, eng, sem, base):
        self.eng, self.sem, self.base, self.n = eng, sem, base, 0

    def __call__(self, ins):
        self.n += 1
        ins.then_inc(self.sem, 1)
        self.eng.wait_ge(self.sem, self.base + self.n)


OWN = {"dveA": 24, "dveC": 27, "dveE": 12, "actA": 8, "actC": 3, "actE": 1}


def own_base(eng, ph, i):
    before = sum(OWN[eng + q] * TURNS for q in "ACE"[:"ACE".index(ph)])
    return i * OWN[eng + ph] + before


SCORES0 = 2 * GH * 2 - 7
TURNED0 = 13
BEFORE = {"C": 0, "E": B // PAIR * EU}
OT0 = 1
XC0 = 1
QUOT0 = 3
PV0 = 2
DOWN0 = 4
STORED = 2 * SPLITS * 16
STACK = 2 * SPLITS * SPLITS * 16


class At:

    def __init__(self, turn, L):
        self.place = turn * 2
        self.turn = turn + LAYER[L] * (HEADS // UNROLL)
        self.group, self.head = self.turn * 2, self.turn * UNROLL


def build(nc, xT, cT, wmod, wqkv, bqkv, alpha, wo0, bo0, gwT, gb, rms, w1, b1, w2, b2,
          l1w, l1down, l1up, l1wo, mw1, mb1, mw2, mb2, scale, ident_in, blk_in, decay_in,
          parts, x1, out):
    ctx = ExitStack()
    with ctx:
        def sb(name, shape, dt=F32):
            return ctx.enter_context(nc.sbuf_tensor(name, shape, dt))

        sems = {}

        def sem(name):
            if name not in sems:
                sems[name] = ctx.enter_context(nc.semaphore(name))
            return sems[name]

        vall = sb("vall", [P, GROUPS, NT, GH, VC])
        vg = sb("vg", [P, 2, NT, GH, 32])
        oall = sb("oall", [P, GROUPS, NT, GH * DH])
        qst = sb("qst", [P, 2, GH, S], BF16)
        kst = sb("kst", [P, 2, GH, S], BF16)
        decay = sb("decay", [P, NT, S])
        big = sb("big", [P, 56 * S])
        small = sb("small", [P, 64])
        mod = sb("mod", [P, B, 12])
        mbs = sb("mbs", [P, PAIR, 12])
        ident = sb("ident", [P, P])
        mean_w = sb("mean_w", [P, P])
        ones = sb("ones", [P, P])
        blk = sb("blk", [P, P])
        wmod_sb = big[:, 46 * S:49 * S].rearrange("p (l m) -> p l m", l=2)
        c_sb = sb("c_sb", [P, 2, B])
        sil = sb("sil", [P, 4, 2, B])
        w_qkv = sb("w_qkv", [P, 3, D])
        b_qkv = sb("b_qkv", [P, 3])
        al = sb("al", [P, 3])
        s_base = sb("s_base", [P, 3])
        s_yat = sb("s_yat", [P, 3])
        wn = sb("wn", [P, 3])
        wo0_sb = sb("wo0_sb", [P, D])
        bo0_sb = sb("bo0_sb", [P, 1])
        gw_sb = sb("gw_sb", [P, EX])
        gb_sb = sb("gb_sb", [P, EX])
        rms_sb = sb("rms_sb", [P, EX])
        w1_sb = big[:, 46 * S:50 * S].rearrange("p (u c) -> p u c", u=EU)
        b1_sb = sb("b1_sb", [P, EU])
        w2_sb = big[:, 50 * S:54 * S].rearrange("p (u c) -> p u c", u=EU)
        b2_sb = sb("b2_sb", [P, EX])
        b2s = sb("b2s", [P, 1])
        l1w_sb = sb("l1w_sb", [P, 3, D])
        dn_sb = sb("dn_sb", [P, 32])
        up_sb = sb("up_sb", [32, 2, D])
        wo1_sb = sb("wo1_sb", [P, D])
        mw1_sb = sb("mw1_sb", [P, MH])
        mb1_sb = sb("mb1_sb", [P, MU])
        mw2_sb = sb("mw2_sb", [P, MU, D])
        mb2_sb = sb("mb2_sb", [P, 1])
        sc_sb = sb("sc_sb", [P, 1])
        ps = ctx.enter_context(nc.psum_tensor("ps", [P, 8, 512], F32))

        HS = NT * S
        Y = [big[:, n * HS:(n + 1) * HS] for n in range(4)]
        A = [big[:, (4 + n) * HS:(5 + n) * HS] for n in range(2)]
        PT = [big[:, (6 + 4 * n) * HS:(10 + 4 * n) * HS].rearrange("p (j t s) -> p j t s", j=GH, t=NT)
              for n in range(2)]

        class Work:

            def __init__(self, p):
                self.p = p
                self.mb = mbs[:, p, :]
                self.ev = evs[:, p]
                self.tiny = tinies[:, p, :]

                def at(*slots):
                    for n in slots:
                        yield big[:, (23 * p + n) * S:(23 * p + n + 1) * S]

                self.xb, self.xc, self.sq, self.t, self.h = at(0, 1, 2, 5, 6)
                self.y, self.xin, self.os = at(14, 4, 3)
                self.rest = list(at(14, 18))
                self.vs, self.rs, self.ts = (self.tiny[:, 32 + 4 * n:36 + 4 * n] for n in range(3))
                self.nv, self.c, self.cs = (self.tiny[:, 44 + NT * H * n:44 + NT * H * (n + 1)] for n in range(3))
                self.q, self.k, self.vv, self.n2, self.qq, self.kk, self.cx = at(7, 8, 9, 17, 15, 16, 17)
                self.d, self.yd, self.z = list(at(10, 11, 12)), list(at(3, 4, 13)), list(at(14, 18, 5))
                self.oT, self.ao, self.kv, self.lat = at(11, 12, 10, 11)
                self.g = list(at(7, 8, 9, 13))
                self.w1e, self.w2e, self.evm, self.ev2, self.res = at(15, 16, 17, 18, 12)
                pair = lambda n: big[:, (23 * p + n) * S:(23 * p + n) * S + SPLITS * S // 2].bitcast(BF16)\
                    .rearrange("p (a s) -> p a s", a=SPLITS)
                self.pq, self.pk = pair(19), pair(21)

            def bank(self, n):
                return ps[:, 4 * self.p + n, :]

            def sem(self, ph, name):
                return sem(f"{ph}{self.p}_{name}")

        tinies = sb("tinies", [P, PAIR, 44 + 3 * NT * H])
        evs = sb("evs", [32, PAIR, 2, P])
        work = [Work(p) for p in range(PAIR)]

        pvs = sb("pvs", [P, 2, S])
        mx = sb("mx", [P, 4, NT])
        nb = sb("nb", [P, 4, NT])
        rec = sb("rec", [P, 2, NT * GH])

        def bank(n):
            return ps[:, n, :]

        block = ctx.enter_context(nc.Block())

        def wait_apart(eng, s, value):
            if not isinstance(value, int):
                value = eng.to_reg(value)
            eng.wait_ge(sem("loaded"), LOADED)
            eng.wait_ge(s, value)

        def in_turns(*steps):
            for _ in zip_longest(*steps):
                pass

        def norm_mean(w):
            nc.tensor.matmul(w.bank(0), mean_w[:, :], w.xb, start=True, stop=True)\
              .then_inc(w.sem("N", "mean"), 1)

        def norm_var(pe, w, n):
            pe.wait_ge(w.sem("N", "sq"), n + 1)
            for t in range(NT):
                last = nc.tensor.matmul(w.bank(1)[:, t:t + 1], w.sq[:, t * P:(t + 1) * P], mean_w[:, 0:1],
                                        start=True, stop=True)
            last.then_inc(w.sem("N", "var"), 1)

        def spread(src, dst):
            for t in range(NT):
                last = nc.tensor.matmul(dst[:, t * P:(t + 1) * P], src(t), ident[:, :], start=True, stop=True)
            return last

        def norm_spread(pe, w, n):
            pe.wait_ge(w.sem("N", "rs"), n + 1)
            spread(lambda t: w.rs[:, t:t + 1].broadcast_to([P, P]), w.bank(1))\
              .then_inc(w.sem("N", "rb"), 1)

        def norm_pe(pe, w, n):
            pe.wait_ge(w.sem("N", "x"), n + (1 - TURNS))
            norm_mean(w)
            yield
            norm_var(pe, w, n)
            yield
            norm_spread(pe, w, n)
            yield

        def norm_act(act, own, w, n):
            act.wait_ge(w.sem("N", "xc"), n + 1 + XC0)
            nc.scalar.activation(w.sq, w.xc, ACT.Square).then_inc(w.sem("N", "sq"), 1)
            yield
            act.wait_ge(w.sem("N", "v"), n + 1)
            own(nc.scalar.activation(w.rs, w.vs, ACT.Ln))
            nc.scalar.activation(w.rs, w.rs, ACT.Exp, scale=-0.5).then_inc(w.sem("N", "r"), 1)
            yield

        def newton(own, v, r, t, done, to=None):
            own(nc.vector.tensor_tensor(t, r, r, ALU.mult))
            own(nc.vector.tensor_tensor(t, t, v, ALU.mult))
            own(nc.vector.tensor_scalar(t, t, -0.5, 1.5, ALU.mult, ALU.add))
            if done is None:
                own(nc.vector.tensor_tensor(r, r, t, ALU.mult))
            elif to is None:
                nc.vector.tensor_tensor(r, r, t, ALU.mult).then_inc(done, 1)
            else:
                wide = lambda a: a.unsqueeze(2).broadcast_to([P, NT * H, DH])
                nc.vector.tensor_tensor(to.rearrange("p (n d) -> p n d", d=DH), wide(r), wide(t), ALU.mult)\
                  .then_inc(done, 1)

        def norm_dve(dve, own, w, n, shift, gain):
            dve.wait_ge(w.sem("N", "mean"), n + 1)
            nc.vector.tensor_tensor(w.xc, w.xb, w.bank(0), ALU.subtract).then_inc(w.sem("N", "xc"), 1)
            yield
            dve.wait_ge(w.sem("N", "var"), n + 1)
            nc.vector.tensor_scalar(w.vs, w.bank(1)[:, 0:NT], LN_EPS, None, ALU.add).then_inc(w.sem("N", "v"), 1)
            yield
            dve.wait_ge(w.sem("N", "r"), n + 1)
            newton(own, w.vs, w.rs, w.ts, w.sem("N", "rs"))
            yield
            dve.wait_ge(w.sem("N", "rb"), n + 1)
            own(nc.vector.tensor_tensor(w.h, w.xc, w.bank(1), ALU.mult))
            nc.vector.tensor_scalar(w.h, w.h, w.mb[:, gain:gain + 1], w.mb[:, shift:shift + 1],
                                    ALU.mult, ALU.add).then_inc(w.sem("N", "h"), 1)
            yield

        def split_act(act, ph, w, i, which, src, dst, done):
            before = 4 * TURNS * "AC".index(ph) + 2 * which
            for part in range(SPLITS):
                if part:
                    act.wait_ge(w.sem("N", "rest"), i * 4 + (before + part))
                ins = nc.scalar.activation(dst[:, part, :], w.rest[which] if part else src, ACT.Copy)
                ins.then_inc(done if part == SPLITS - 1 else w.sem("N", "part"), 1)
                yield

        def split_dve(dve, ph, w, i, which, src, dst):
            before = 4 * TURNS * "AC".index(ph) + 2 * which
            for part in range(SPLITS - 1):
                dve.wait_ge(w.sem("N", "part"), i * 4 + (before + part + 1))
                nc.vector.tensor_tensor(w.rest[which], w.rest[which] if part else src, dst[:, part, :],
                                        ALU.subtract).then_inc(w.sem("N", "rest"), 1)
                yield

        def store_parts(sp, ph, w, i, o, last):
            wait_apart(sp, w.sem(ph, ("pq", "pk")[o]), i + 1 + last)
            for a in range(SPLITS):
                dst = parts["AC".index(ph), o, bass.ds(i * PAIR + w.p, 1), :, a, :, :]
                sp.dma_start(dst.rearrange("o h d t -> (o h) d t"), (w.pq, w.pk)[o][:, a, :])\
                  .then_inc(w.sem("N", "stored"), 16)

        def parts_stored(eng, ph):
            for w in work:
                eng.wait_ge(w.sem("N", "stored"), 16 + TURNS * STORED * ("AC".index(ph) + 1))

        def load_x(sp, src, dst, w, i, norms):
            wait_apart(sp, w.sem("N", "xc"), norms)
            sp.dma_start(dst, src[:, bass.ds((i * PAIR + w.p) * S, S)]).then_inc(w.sem("N", "load"), 16)

        def values_to_groups(own, w, i, n):
            by = w.bank(n).rearrange("p (t g j d) -> p g t j d", t=NT, g=NG, j=GH)
            for g in range(NG):
                own(nc.vector.tensor_copy(vall[:, bass.ds(i * (PAIR * NG) + (w.p * NG + g), 1), :, :, 0:DH]
                                          .rearrange("p o t j d -> p (o t) j d"), by[:, g]))

        def batch_in_pool(pool, ph, w, i, done, with_out):
            if with_out:
                wait_apart(pool, w.sem("O", "oT"), i + (TURNS * (ph == "E") + OT0))
                for g in range(NG):
                    nc.gpsimd.tensor_copy(
                        w.os.rearrange("p (t g c) -> p t g c", t=NT, g=NG)[:, :, g, :],
                        oall[:, bass.ds(i * (PAIR * NG) + (w.p * NG + g), 1), :, :].rearrange("p o t c -> p (o t) c"))\
                      .then_inc(w.sem("O", "os"), 1)
            wait_apart(pool, done, i + 1)
            nc.gpsimd.tensor_copy(w.mb, mod[:, bass.ds(i * PAIR + w.p, 1), :].rearrange("p o m -> p (o m)"))\
              .then_inc(w.sem("N", "mb"), 1)

        def attn_out_pe(pe, ph, w, i, n, wo):
            pe.wait_ge(w.sem("O", "os"), n * NG + NG)
            for t in range(NT):
                last = nc.tensor.transpose(w.bank(0)[:, t * P:(t + 1) * P], w.os[:, t * P:(t + 1) * P],
                                           ident[:, :])
            last.then_inc(w.sem("O", "oT"), 1)
            yield
            pe.wait_ge(w.sem("O", "oTs"), n + 1)
            nc.tensor.matmul(w.bank(1), wo[:, :], w.oT, start=True, stop=True)\
              .then_inc(w.sem("O", "ao"), 1)
            yield

        def attn_out_dve(dve, own, ph, w, i, n, bias, gate):
            dve.wait_ge(w.sem("O", "oT"), n + (1 + OT0))
            nc.vector.tensor_copy(w.oT, w.bank(0)).then_inc(w.sem("O", "oTs"), 1)
            yield
            dve.wait_ge(w.sem("N", "mb"), i + (TURNS * "ACE".index(ph) + 1))
            dve.wait_ge(w.sem("N", "load"), i * 16 + (TURNS * "ACE".index(ph) + 1) * 16)
            dve.wait_ge(w.sem("O", "ao"), n + 1)
            if bias is None:
                nc.vector.scalar_tensor_tensor(w.xb, w.bank(1), w.mb[:, gate:gate + 1], w.xin, ALU.mult, ALU.add)\
                  .then_inc(w.sem("N", "x"), 1)
            else:
                own(nc.vector.tensor_scalar(w.ao, w.bank(1), bias, w.mb[:, gate:gate + 1], ALU.add, ALU.mult))
                dve.wait_ge(w.sem("C", "xst"), i * 16 + 16)
                nc.vector.tensor_tensor(w.xb, w.xin, w.ao, ALU.add).then_inc(w.sem("N", "x"), 1)
            yield

        def mlp_pe(pe, ph, w, i, n, up, down):
            def rise(u):
                if u >= 2:
                    pe.wait_ge(w.sem("O", "gelu"), i * n + (BEFORE[ph] + u - 1))
                nc.tensor.matmul(w.bank(u % 2), up(u), w.h, start=True, stop=True)\
                  .then_inc(w.sem("O", "up"), 1)
            rise(0)
            rise(1)
            yield
            if ph == "E":
                pe.wait_ge(w.sem("E", "weights"), i * 2 + 2)
            for u in range(n):
                if u + 2 < n:
                    rise(u + 2)
                pe.wait_ge(w.sem("O", "gelu"), i * n + (BEFORE[ph] + u + 1))
                nc.tensor.matmul(w.bank(2), down(u), w.g[u % 4], start=(u == 0), stop=(u == n - 1))\
                  .then_inc(w.sem("O", "down"), 1)
                yield

        def mlp_act(act, ph, w, i, n, bias):
            for u in range(n):
                act.wait_ge(w.sem("O", "down"), i * n + (BEFORE[ph] + u + 1))
                act.wait_ge(w.sem("O", "up"), i * n + (BEFORE[ph] + u + 1))
                nc.scalar.activation(w.g[u % 4], w.bank(u % 2), ACT.Gelu, bias=bias[:, u:u + 1])\
                  .then_inc(w.sem("O", "gelu"), 1)
                yield

        def each_slot(eng, L, slot, late=0):
            for turn in range(FILL):
                for s in range(UNROLL):
                    slot(s, At(turn, L), lambda n, turn=turn: turn * UNROLL + n >= 0)
            with eng.Fori(FILL, HEADS // UNROLL) as i:
                at = At(i, L)
                for s in range(UNROLL):
                    slot(s, at, lambda n: True)
            end = At(HEADS // UNROLL, L)
            for s in range(LAG[L] + OUT_LAG + late):
                slot(s, end, lambda n: n < 0)

        def stacks(sp, L, i):
            src_of = [parts[LAYER[L], o].rearrange("b (g j) a d t -> (b g) j a d t", g=NG) for o in range(2)]
            for g in range(2):
                sp.wait_ge(sem("scores"), At(i, L).head * 2 + (8 * g + 1))
                for a in range(SPLITS):
                    for r in range(SPLITS):
                        row = (a * SPLITS + r) * DH
                        for o, st, part in ((0, qst, r), (1, kst, a)):
                            src = src_of[o][bass.ds(i * 2 + g, 1), :, part, :, :]
                            sp.dma_start(st[row:row + DH, g, :, :], src.rearrange("o j d t -> d (o j) t"))\
                              .then_inc(sem(f"stack{g}"), 16)

        def first_stacks(sp, L):
            sp.wait_ge(work[0].sem("N", "stored"), 16 + STORED * (TURNS * LAYER[L] + 1))
            stacks(sp, L, 0)

        def attn_sp(sp, L):
            with sp.Fori(1, GROUPS // 2) as i:
                stacks(sp, L, i)

        def attn_pool(pool, L):
            with pool.Fori(0, GROUPS // 2) as i:
                for g in range(2):
                    wait_apart(pool, sem("pv"), At(i, L).group + (g + 1))
                    nc.gpsimd.tensor_copy(
                        vg[:, g, :, :, 0:VC],
                        vall[:, bass.ds(i * 2 + g, 1), :, :, :].rearrange("p o t j c -> p (o t) j c"))\
                      .then_inc(sem("vg"), 1)

        def attn_pe(pe, L, wait_read):
            def scores(n, chunks, at):
                par = (n // GH) % 2
                if n % GH == 0 and chunks[0] == 0:
                    pe.wait_ge(sem(f"stack{par}"), at.turn * STACK + STACK)
                for c in chunks:
                    wait_read(n, c, at)
                    for t in (2 * c, 2 * c + 1):
                        last = nc.tensor.matmul(bank(t), qst[:, par, n % GH, t * P:(t + 1) * P],
                                                kst[:, par, n % GH, :], start=True, stop=True)
                    last.then_inc(sem("scores"), 1)

            def transposes(n, kts, at):
                if kts[0] == 0:
                    pe.wait_ge(sem("probs"), at.head + (n + 1))
                for kt in kts:
                    pe.wait_ge(sem(f"evac{kt % 2}"), at.head * 2 + (2 * n + kt // 2 + 1))
                    for t in range(NT):
                        last = nc.tensor.transpose(ps[:, 4 + kt % 2, t * P:(t + 1) * P],
                                                   Y[n % 4][:, t * S + kt * P:t * S + (kt + 1) * P], ident[:, :])
                    last.then_inc(sem("turned"), 1)

            def values(n, kt, at):
                g, par = n // GH, (n // GH) % 2
                if kt == 0:
                    for k in range(2):
                        pe.wait_ge(sem(f"evac{k}"), at.head * 2 + (8 * g + 9))
                    pe.wait_ge(sem("vg"), at.group + (g + 1))
                    pe.wait_ge(sem("pvs"), at.group + (g + 1))
                for j in range(GH):
                    last = nc.tensor.matmul(ps[32 * j:32 * j + 32, 6, :], vg[:, par, kt, j, :], PT[par][:, j, kt, :],
                                            start=(kt == 0), stop=(kt == NT - 1))
                if kt == NT - 1:
                    last.then_inc(sem("pv"), 1)

            def by_token(n, at):
                g, par = n // GH, (n // GH) % 2
                pe.wait_ge(sem("pvs"), at.group + (g + 2))
                pe.wait_ge(sem("out"), at.group + (g + 1))
                for t in range(NT):
                    last = nc.tensor.transpose(ps[:, 7, t * P:(t + 1) * P], pvs[:, par, t * P:(t + 1) * P],
                                               ident[:, :])
                last.then_inc(sem("pvT"), 1)

            def slot(s, at, on):
                n = s - LAG[L] - 1
                if on(n):
                    transposes(n, (0, 1), at)
                if on(s):
                    scores(s, (0, 1) if L == "B" else (0,), at)
                if on(n):
                    transposes(n, (2, 3), at)
                if n % GH == 1 and on(n - n % GH - 2 * GH):
                    by_token(n - n % GH - 2 * GH, at)
                if on(n - GH):
                    values(n - GH, n % GH, at)
                if on(s) and L == "D":
                    scores(s, (1,), at)
            each_slot(pe, L, slot, 1)

        def group_out_dve(dve, L, n, at, on):
            m = n - n % GH - 2 * GH
            g, par = m // GH, (m // GH) % 2
            if n % GH == 0 and on(m) and L == "B":
                dve.wait_ge(sem("pv"), at.group + (g + 1 + PV0))
                nc.vector.tensor_copy(pvs[:, par, :], bank(6)).then_inc(sem("pvs"), 1)
            if n % GH == 2 and on(m):
                dve.wait_ge(sem("pvT"), at.group + (g + 1))
                by = bank(7).rearrange("p (m c) -> p m c", c=32)
                nc.vector.reciprocal(rec[:, par, :], by[:, :, DH]).then_inc(sem("rec"), 1)
                dve.wait_ge(sem("rec"), at.group + (g + 1))
                dst = oall[:, bass.ds(at.place + g, 1), :, :].rearrange("p o t (j d) -> p (o t j) d", d=DH)
                nc.vector.tensor_tensor(dst, by[:, :, 0:DH],
                                        rec[:, par, :].unsqueeze(2).broadcast_to([P, NT * GH, DH]), ALU.mult)\
                  .then_inc(sem("out"), 1)

        def attn1_act(act):
            def exponential(n, t):
                sl = Y[n % 4][:, t * S:(t + 1) * S]
                return nc.scalar.activation(sl, sl, ACT.Exp, bias=nb[:, n % 4, t:t + 1], scale=0.5)

            def slot(s, at, on):
                if on(s):
                    act.wait_ge(sem("turned"), at.head * 4 + (4 * s + 1))
                    for c in range(2):
                        act.wait_ge(sem("scores"), at.head * 2 + (2 * s + c + 1 + SCORES0))
                        nc.scalar.activation(Y[s % 4][:, c * 2 * S:(c + 1) * 2 * S],
                                             ps[:, 2 * c:2 * c + 2, :].rearrange("p a s -> p (a s)"),
                                             ACT.Square).then_inc(sem("scored"), 1)
                n = s - 1
                if on(n):
                    act.wait_ge(sem("abs"), at.head + (n + 1))
                    nc.scalar.activation(A[n % 2], A[n % 2], ACT.Ln).then_inc(sem("ln"), 1)
                if on(s - 2):
                    act.wait_ge(sem("bias"), at.head + (s - 1))
                    exponential(s - 2, 0)
                if on(n):
                    act.wait_ge(sem("ln"), at.head + (n + 1))
                    nc.scalar.activation(A[n % 2], A[n % 2], ACT.Exp, scale=-2.0).then_inc(sem("inv"), 1)
                n = s - 2
                if on(n):
                    for t in range(1, NT):
                        last = exponential(n, t)
                    last.then_inc(sem("probs"), 1)
            each_slot(act, "B", slot)

        def attn1_dve(dve):
            def evac(n, kt, at):
                dve.wait_ge(sem("turned"), at.head * 4 + (4 * n + kt + 1 + TURNED0))
                nc.vector.tensor_copy(PT[(n // GH) % 2][:, n % GH, kt, :], bank(4 + kt % 2))\
                  .then_inc(sem(f"evac{kt % 2}"), 1)

            def slot(s, at, on):
                if on(s):
                    dve.wait_ge(sem("scored"), at.head * 2 + (2 * s + 4))
                    nc.vector.tensor_scalar(Y[s % 4], Y[s % 4], 1.0, ZERO_GUARD, ALU.subtract, ALU.subtract)\
                      .then_inc(sem("den"), 1)
                    dve.wait_ge(sem("den"), at.head + (s + 1))
                    nc.vector.tensor_scalar(A[s % 2].bitcast(U32), Y[s % 4].bitcast(U32), 0x7fffffff, None,
                                            ALU.bitwise_and).then_inc(sem("abs"), 1)
                n, m = s - 1, s - 3
                group_out_dve(dve, "B", m, at, on)
                if on(m):
                    evac(m, 0, at)
                    evac(m, 1, at)
                for t in range(NT):
                    if on(n):
                        if t == 0:
                            wait_apart(dve, sem("inv"), at.head + (n + 1))
                        sl = slice(t * S, (t + 1) * S)
                        nc.vector.tensor_tensor_reduce(out=Y[n % 4][:, sl], in0=Y[n % 4][:, sl], in1=A[n % 2][:, sl],
                                                       scale=-1.0, scalar=-3e38, op0=ALU.mult, op1=ALU.max,
                                                       accum_out=mx[:, n % 4, t:t + 1]).then_inc(sem("quot"), 1)
                    if on(m) and t in (1, 2):
                        evac(m, t + 1, at)
                if on(n):
                    dve.wait_ge(sem("quot"), at.head * 4 + (4 * n + 4 + QUOT0))
                    nc.vector.tensor_scalar(nb[:, n % 4, :], mx[:, n % 4, :], -0.5, None, ALU.mult)\
                      .then_inc(sem("bias"), 1)
            each_slot(dve, "B", slot)

        def by_scalar(n, kt):
            return n % GH == 2 and kt == 2

        def attn2_act(act):
            def slot(s, at, on):
                for t in range(NT):
                    n = s - 1
                    if on(n):
                        if t == 0:
                            act.wait_ge(sem("bias"), at.head + (n + 1))
                        sl = Y[n % 4][:, t * S:(t + 1) * S]
                        ins = nc.scalar.activation(sl, sl, ACT.Exp, bias=nb[:, n % 4, t:t + 1], scale=DOT_SCALE)
                        if t == NT - 1:
                            ins.then_inc(sem("probs"), 1)
                    m = s - 2 - 2 * GH
                    if t == 0 and m % GH == 0 and on(m):
                        g = m // GH
                        act.wait_ge(sem("pv"), at.group + (g + 1 + PV0))
                        nc.scalar.activation(pvs[:, g % 2, :], bank(6), ACT.Copy).then_inc(sem("pvs"), 1)
                    n = s - 2
                    if on(n) and (t % 2 or by_scalar(n, t)):
                        act.wait_ge(sem("turned"), at.head * 4 + (4 * n + t + 1 + TURNED0))
                        nc.scalar.activation(PT[(n // GH) % 2][:, n % GH, t, :], bank(4 + t % 2), ACT.Copy)\
                          .then_inc(sem(f"evac{t % 2}"), 1)
            each_slot(act, "D", slot)

        def attn2_dve(dve):
            def slot(s, at, on):
                for t in range(NT):
                    if on(s):
                        if t == 0:
                            dve.wait_ge(sem("turned"), at.head * 4 + (4 * s + 1))
                        wait_apart(dve, sem("scores"), at.head * 2 + (2 * s + t // 2 + 1 + SCORES0))
                        nc.vector.tensor_tensor_reduce(out=Y[s % 4][:, t * S:(t + 1) * S], in0=bank(t),
                                                       in1=decay[:, t, :],
                                                       scale=1.0, scalar=-3e38, op0=ALU.mult, op1=ALU.max,
                                                       accum_out=mx[:, s % 4, t:t + 1]).then_inc(sem("quot"), 1)
                    n = s - 2
                    if on(n) and t % 2 and not by_scalar(n, t - 1):
                        dve.wait_ge(sem("turned"), at.head * 4 + (4 * n + t + TURNED0))
                        nc.vector.tensor_copy(PT[(n // GH) % 2][:, n % GH, t - 1, :], bank(4)).then_inc(sem("evac0"), 1)
                if on(s):
                    dve.wait_ge(sem("quot"), at.head * 4 + (4 * s + 4 + QUOT0))
                    nc.vector.tensor_scalar(nb[:, s % 4, :], mx[:, s % 4, :], -DOT_SCALE, None, ALU.mult)\
                      .then_inc(sem("bias"), 1)
                group_out_dve(dve, "D", s - 2, at, on)
            each_slot(dve, "D", slot)

        loads = [(c_sb[:, :, :], cT), (wmod_sb[:, :, :], wmod), (mean_w[:, :], blk_in[:, 0, :]),
                 (ident[:, :], ident_in), (blk[:, :], blk_in[:, 1, :]), (ones[:, :], blk_in[:, 2, :]),
                 (w_qkv[:, :, :], wqkv), (b_qkv[:, :], bqkv), (al[:, :], alpha.partition_broadcast(P)),
                 (b2_sb[:, :], b2)]
        later = [(decay[:, :, :], decay_in), (wo0_sb[:, :], wo0), (bo0_sb[:, :], bo0), (gw_sb[:, :], gwT),
                 (gb_sb[:, :], gb.partition_broadcast(P)), (rms_sb[:, :], rms.partition_broadcast(P)),
                 (b1_sb[:, :], b1),
                 (l1w_sb[:, :, :], l1w), (dn_sb[:, :], l1down), (up_sb[:, :, :], l1up), (wo1_sb[:, :], l1wo),
                 (mw1_sb[:, :], mw1), (mb1_sb[:, :], mb1), (mw2_sb[:, :, :], mw2), (mb2_sb[:, :], mb2),
                 (sc_sb[:, :], scale.partition_broadcast(P))]
        LOADED = 16 * len(loads)
        ALL_LOADED = LOADED + 16 * len(later)

        @block.sync
        def _(sp):
            for dst, src in loads:
                sp.dma_start(dst, src).then_inc(sem("loaded"), 16)

            def a_load(w, i):
                load_x(sp, xT, w.xb, w, i, i + XC0)

            def c_load(w, i):
                load_x(sp, xT, w.xin, w, i, i * 2 + (TURNS - 1 + XC0))

            def each_turn(turn, L):
                with sp.Fori(0, TURNS - 1) as i:
                    turn(i, True)
                first_stacks(sp, L)
                turn(TURNS - 1, False)

            def a_turn(i, more):
                for w in work:
                    store_parts(sp, "A", w, i, 1, 0)
                if more:
                    for w in work:
                        a_load(w, i + 1)
                for w in work:
                    store_parts(sp, "A", w, i, 0, 1)
            for w in work:
                a_load(w, 0)
            sp.wait_ge(sem("zeros"), 4)
            each_turn(a_turn, "B")
            for dst, src in later:
                sp.dma_start(dst, src).then_inc(sem("loaded"), 16)
            parts_stored(sp, "A")
            attn_sp(sp, "B")
            sp.wait_ge(sem("out"), GROUPS + 1)
            sp.dma_start(w1_sb, w1).then_inc(sem("experts"), 16)
            sp.dma_start(w2_sb, w2).then_inc(sem("experts"), 16)

            def c_turn(i, more):
                for w in work:
                    wait_apart(sp, w.sem("N", "x"), i * 2 + 2)
                    sp.dma_start(x1[:, bass.ds((i * PAIR + w.p) * S, S)], w.xb).then_inc(w.sem("C", "xst"), 16)
                for w in work:
                    store_parts(sp, "C", w, i, 0, 0)
                if more:
                    for w in work:
                        c_load(w, i + 1)
                for w in work:
                    store_parts(sp, "C", w, i, 1, 1)
            for w in work:
                c_load(w, 0)
            each_turn(c_turn, "D")
            parts_stored(sp, "C")
            for w in work:
                sp.wait_ge(w.sem("C", "xst"), 16 + 16 * TURNS)
            attn_sp(sp, "D")
            sp.wait_ge(sem("out"), 2 * GROUPS + 1)
            with sp.Fori(0, TURNS) as i:
                for w in work:
                    load_x(sp, x1, w.xin, w, i, i + (3 * TURNS + XC0))
                for w in work:
                    sp.wait_ge(w.sem("E", "res"), i + 2)
                    sp.dma_start(out[:, bass.ts(i * PAIR + w.p, S)], w.res).then_inc(w.sem("E", "outd"), 16)
            for w in work:
                sp.wait_ge(w.sem("E", "outd"), 16 + 16 * TURNS)

        @block.gpsimd
        def _(pool):
            first = [("scored", 2), ("quot", QUOT0), ("turned", TURNED0), ("scores", SCORES0), ("pv", PV0),
                     ("pvs", 1), ("out", 1), ("evac0", 1), ("evac1", 1)]
            for p in range(PAIR):
                first += [(f"O{p}_oT", OT0), (f"N{p}_xc", XC0), (f"A{p}_pq", 1), (f"C{p}_pk", 1), (f"E{p}_res", 1), (f"N{p}_stored", 16),
                          (f"C{p}_xst", 16), (f"E{p}_outd", 16),
                          (f"O{p}_down", DOWN0)]
            for n, (name, count) in enumerate(first):
                nc.gpsimd.memset(small[:, n:n + 1], 0.0).then_inc(sem(name), count)
            nc.gpsimd.memset(s_base[:, :], YAT_BASE).then_inc(sem("base"), 1)
            nc.gpsimd.memset(vg[:, :, :, :, :], 0.0).then_inc(sem("zeros"), 1)
            nc.gpsimd.memset(vall[:, :, :, :, DH:VC], 1.0).then_inc(sem("zeros"), 1)
            pool.wait_ge(sem("loaded"), LOADED)
            pool.wait_ge(sem("base"), 1)
            nc.gpsimd.tensor_tensor(s_yat[:, :], s_base[:, :], al[:, :], ALU.pow).then_inc(sem("yat"), 1)
            pool.wait_ge(sem("mod"), 1)
            with pool.Fori(0, TURNS) as i:
                for w in work:
                    batch_in_pool(pool, "A", w, i, w.sem("A", "pq"), False)
            for w in work:
                pool.wait_ge(w.sem("A", "pq"), TURNS + 1)
            pool.wait_ge(sem("zeros"), 4)
            attn_pool(pool, "B")
            pool.wait_ge(sem("out"), GROUPS + 1)
            with pool.Fori(0, TURNS) as i:
                for w in work:
                    batch_in_pool(pool, "C", w, i, w.sem("C", "pk"), True)
            for w in work:
                pool.wait_ge(w.sem("C", "pk"), TURNS + 1)
            attn_pool(pool, "D")
            pool.wait_ge(sem("out"), 2 * GROUPS + 1)
            with pool.Fori(0, TURNS) as i:
                for w in work:
                    batch_in_pool(pool, "E", w, i, w.sem("E", "res"), True)

        def first_guess(act, own, ready, v, r, done, i):
            act.wait_ge(ready, i + 1)
            own(nc.scalar.activation(r, v, ACT.Ln))
            nc.scalar.activation(r, r, ACT.Exp, scale=-0.5).then_inc(done, 1)

        def a_act(act, w, i):
            own = Order(act, w.sem("N", "act"), own_base("act", "A", i))
            yield from norm_act(act, own, w, i)
            act.wait_ge(w.sem("N", "h"), i + 1)
            nc.scalar.activation(w.sq, w.h, ACT.Square).then_inc(w.sem("A", "h2"), 1)
            act.wait_ge(w.sem("A", "dot"), i + 1)
            for j in range(3):
                nc.scalar.activation(w.d[j], w.bank(1 + j), ACT.Square, scale=0.5)\
                  .then_inc(w.sem("A", "d2"), 1)
            yield
            for j in range(3):
                act.wait_ge(w.sem("A", "y"), i * 3 + (j + 1))
                own(nc.scalar.activation(w.z[j], w.yd[j], ACT.Square))
                own(nc.scalar.activation(w.z[j], w.z[j], ACT.Ln))
                nc.scalar.activation(w.z[j], w.z[j], ACT.Exp, scale=-1.0).then_inc(w.sem("A", "z"), 1)
                yield
            act.wait_ge(w.sem("A", "qkv"), i * 4 + 1)
            nc.scalar.activation(w.qq, w.q, ACT.Square).then_inc(w.sem("A", "qq"), 1)
            act.wait_ge(w.sem("A", "qkv"), i * 4 + 2)
            nc.scalar.activation(w.kk, w.k, ACT.Square).then_inc(w.sem("A", "qq"), 1)
            yield
            first_guess(act, own, w.sem("A", "nv"), w.nv, w.c, w.sem("A", "c"), i)
            yield
            act.wait_ge(w.sem("N", "stored"), i * STORED + 16)
            yield from split_act(act, "A", w, i, 0, w.k, w.pk, w.sem("A", "pk"))
            act.wait_ge(w.sem("A", "qkv"), i * 4 + 4)
            yield from split_act(act, "A", w, i, 1, w.q, w.pq, w.sem("A", "pq"))
            assert own.n == OWN["actA"]

        def c_act(act, w, i):
            own = Order(act, w.sem("N", "act"), own_base("act", "C", i))
            yield from norm_act(act, own, w, i * 2 + TURNS)
            first_guess(act, own, w.sem("C", "ms"), w.tiny[:, 0:4], w.tiny[:, 4:8], w.sem("C", "rms"), i)
            yield
            yield from mlp_act(act, "C", w, i, EU, b1_sb)
            if w.p == 0:
                nc.scalar.preload_act_table_set("natural_log_exp_and_others")
            act.wait_ge(w.sem("C", "lm"), i + 1)
            nc.scalar.activation(w.t[:, 32:64], w.t[:, 0:32], ACT.Exp, scale=2.0).then_inc(w.sem("C", "le"), 1)
            yield
            yield from norm_act(act, own, w, i * 2 + (TURNS + 1))
            act.wait_ge(w.sem("C", "kvq"), i * 2 + 2)
            act.wait_ge(w.sem("N", "stored"), i * STORED + (TURNS * STORED + 16))
            yield from split_act(act, "C", w, i, 0, w.bank(2), w.pq, w.sem("C", "pq"))
            act.wait_ge(w.sem("C", "rec"), i + 1)
            yield from split_act(act, "C", w, i, 1, w.bank(1), w.pk, w.sem("C", "pk"))
            assert own.n == OWN["actC"]

        def e_act(act, w, i):
            own = Order(act, w.sem("N", "act"), own_base("act", "E", i))
            yield from norm_act(act, own, w, i + 3 * TURNS)
            yield from mlp_act(act, "E", w, i, MU, mb1_sb)
            assert own.n == OWN["actE"]

        @block.scalar
        def _(act):
            act.wait_ge(sem("loaded"), LOADED)
            nc.scalar.preload_act_table_set("natural_log_exp_and_others")
            nc.scalar.activation(sil[:, 0], c_sb[:, :, :], ACT.Exp, scale=-1.0).then_inc(sem("sil_e"), 1)
            with act.Fori(0, TURNS) as i:
                in_turns(*(a_act(act, w, i) for w in work))
            attn1_act(act)
            act.wait_ge(sem("loaded"), ALL_LOADED)
            with act.Fori(0, TURNS) as i:
                nc.scalar.preload_act_table_set("natural_log_exp_and_others")
                in_turns(*(c_act(act, w, i) for w in work))
            nc.scalar.preload_act_table_set("natural_log_exp_and_others")
            attn2_act(act)
            with act.Fori(0, TURNS) as i:
                nc.scalar.preload_act_table_set("natural_log_exp_and_others")
                in_turns(*(e_act(act, w, i) for w in work))

        def a_pe(pe, w, i):
            pe.wait_ge(w.sem("N", "load"), i * 16 + 16)
            norm_mean(w)
            yield
            norm_var(pe, w, i)
            yield
            norm_spread(pe, w, i)
            yield
            pe.wait_ge(w.sem("N", "h"), i + 1)
            for j in range(3):
                last = nc.tensor.matmul(w.bank(1 + j), w_qkv[:, j, :], w.h, start=True, stop=True)
            last.then_inc(w.sem("A", "dot"), 1)
            pe.wait_ge(w.sem("A", "h2"), i + 1)
            nc.tensor.matmul(w.bank(0), ones[:, :], w.sq, start=True, stop=True).then_inc(w.sem("A", "n2"), 1)
            yield
            pe.wait_ge(w.sem("A", "s2"), i + 1)
            for t in range(NT):
                last = nc.tensor.matmul(w.bank(0)[:, t * H:(t + 1) * H], w.qq[:, t * P:(t + 1) * P],
                                        blk[:, bass.DynSlice(0, H, step=DH)], start=True, stop=True)
            last.then_inc(w.sem("A", "nn"), 1)
            yield
            pe.wait_ge(w.sem("A", "qkv"), i * 4 + 3)
            for t in range(NT):
                last = nc.tensor.transpose(w.bank(1)[:, t * P:(t + 1) * P], w.vv[:, t * P:(t + 1) * P], ident[:, :])
            last.then_inc(w.sem("A", "vt"), 1)
            yield
            pe.wait_ge(w.sem("A", "cs"), i + 1)
            spread(lambda t: w.cx[:, t * P:(t + 1) * P], w.bank(2)).then_inc(w.sem("A", "cb"), 1)

        def c_pe(pe, w, i):
            yield from attn_out_pe(pe, "C", w, i, i, wo0_sb)
            yield from norm_pe(pe, w, i * 2 + TURNS)
            pe.wait_ge(w.sem("N", "h"), i * 2 + (TURNS + 1))
            for t in range(NT):
                last = nc.tensor.matmul(w.bank(3)[:, t * EX:(t + 1) * EX], w.h[:, t * P:(t + 1) * P], gw_sb[:, :],
                                        start=True, stop=True)
            last.then_inc(w.sem("C", "lg"), 1)
            yield
            pe.wait_ge(sem("experts"), 32)
            yield from mlp_pe(pe, "C", w, i, EU, lambda u: w1_sb[:, u, :], lambda u: w2_sb[:, u, :])
            pe.wait_ge(w.sem("C", "ng"), i + 1)
            for t in range(NT):
                last = nc.tensor.matmul(w.bank(3)[:, t * P:(t + 1) * P],
                                        w.tiny[:, 12 + t:13 + t].broadcast_to([P, P]), ident[:, :],
                                        start=True, stop=True)
            last.then_inc(w.sem("C", "ngb"), 1)
            yield
            yield from norm_pe(pe, w, i * 2 + (TURNS + 1))
            pe.wait_ge(w.sem("N", "h"), i * 2 + (TURNS + 2))
            nc.tensor.matmul(w.bank(3), l1w_sb[:, 1, :], w.h, start=True, stop=False)
            nc.tensor.matmul(w.bank(3), l1w_sb[:, 2, :], w.h, start=False, stop=True).then_inc(w.sem("C", "kvq"), 1)
            nc.tensor.matmul(w.bank(2), l1w_sb[:, 0, :], w.h, start=True, stop=True).then_inc(w.sem("C", "kvq"), 1)
            yield
            pe.wait_ge(w.sem("C", "copied"), i * 2 + 1)
            nc.tensor.matmul(w.bank(0)[0:32, :], dn_sb[:, :], w.kv, start=True, stop=True).then_inc(w.sem("C", "lat"), 1)
            yield
            pe.wait_ge(w.sem("C", "copied"), i * 2 + 2)
            nc.tensor.matmul(w.bank(1), up_sb[:, 0, :], w.lat[0:32, :], start=True, stop=True)
            for t in range(NT):
                last = nc.tensor.matmul(w.bank(3)[:, t * P:(t + 1) * P], w.lat[0:32, t * P:(t + 1) * P],
                                        up_sb[:, 1, :], start=True, stop=True)
            last.then_inc(w.sem("C", "rec"), 1)

        def e_pe(pe, w, i):
            yield from attn_out_pe(pe, "E", w, i, i + TURNS, wo1_sb)
            yield from norm_pe(pe, w, i + 3 * TURNS)
            pe.wait_ge(w.sem("N", "h"), i + (3 * TURNS + 1))
            for k in range(2):
                last = nc.tensor.transpose(w.bank(2)[0:32, k * P:(k + 1) * P], w.h[:, 1 + k:33 + k], ident[:, :])
            last.then_inc(w.sem("E", "rows"), 1)
            yield
            pe.wait_ge(w.sem("E", "ev"), i * 2 + 1)
            nc.tensor.matmul(w.bank(3), w.ev[:, 1, :], w.evm[0:32, :], start=True, stop=True)\
              .then_inc(w.sem("E", "delta"), 1)
            yield
            pe.wait_ge(w.sem("E", "ev"), i * 2 + 2)
            for t in range(MU):
                last = nc.tensor.matmul(w.bank(2)[:, t * P:(t + 1) * P], w.ev[:, 1, :],
                                        w.ev2[0:32, t * P:(t + 1) * P], start=True, stop=True)
            last.then_inc(w.sem("E", "delta"), 1)
            yield
            pe.wait_ge(w.sem("E", "weights"), i * 2 + 1)
            yield from mlp_pe(pe, "E", w, i, MU, lambda u: w.w1e[:, u * P:(u + 1) * P],
                              lambda u: w.w2e[:, u * P:(u + 1) * P])

        @block.tensor
        def _(pe):
            pe.wait_ge(sem("sil"), 1)
            for l in range(2):
                for m in range(6):
                    last = nc.tensor.matmul(ps[:, 0, (6 * l + m) * B:(6 * l + m + 1) * B],
                                            wmod_sb[:, l, m * D:(m + 1) * D], sil[:, 3, l, :], start=True, stop=True)
            last.then_inc(sem("modps"), 1)
            pe.wait_ge(sem("wsq"), 1)
            for j in range(3):
                last = nc.tensor.matmul(ps[:, 4, j:j + 1], work[0].d[0][:, j * D:(j + 1) * D], ones[:, 0:1],
                                        start=True, stop=True)
            last.then_inc(sem("wn"), 1)
            pe.wait_ge(sem("wns"), 1)
            with pe.Fori(0, TURNS) as i:
                in_turns(*(a_pe(pe, w, i) for w in work))
            pe.wait_ge(sem("zeros"), 4)
            pe.wait_ge(sem("loaded"), ALL_LOADED)
            parts_stored(pe, "A")
            attn_pe(pe, "B", lambda n, c, at: pe.wait_ge(sem("scored"), at.head * 2 + (2 * n + c + 1)))
            with pe.Fori(0, TURNS) as i:
                in_turns(*(c_pe(pe, w, i) for w in work))
            parts_stored(pe, "C")
            attn_pe(pe, "D", lambda n, c, at: pe.wait_ge(sem("quot"), at.head * 4 + (4 * n + 2 * c + 1)))
            with pe.Fori(0, TURNS) as i:
                in_turns(*(e_pe(pe, w, i) for w in work))

        def a_dve(dve, w, i):
            own = Order(dve, w.sem("N", "dve"), own_base("dve", "A", i))
            dve.wait_ge(w.sem("N", "mb"), i + 1)
            dve.wait_ge(w.sem("N", "load"), i * 16 + 16)
            yield from norm_dve(dve, own, w, i, SA, CA)
            dve.wait_ge(w.sem("A", "n2"), i + 1)

            def denominator(j):
                dve.wait_ge(w.sem("A", "d2"), i * 3 + (j + 1))
                nc.vector.scalar_tensor_tensor(w.yd[j], w.bank(1 + j), wn[:, j:j + 1], w.n2, ALU.add, ALU.add)\
                  .then_inc(w.sem("A", "y"), 1)

            def quotient(j):
                y, z = w.yd[j], w.z[j]
                dve.wait_ge(w.sem("A", "z"), i * 3 + (j + 1))
                own(nc.vector.tensor_tensor(z, y, z, ALU.mult))
                own(nc.vector.tensor_tensor(y, y, z, ALU.mult))
                own(nc.vector.scalar_tensor_tensor(z, y, 2.0, z, ALU.subtract, ALU.mult))
                own(nc.vector.scalar_tensor_tensor(y, w.d[j], -1.0, z, ALU.mult, ALU.mult))
                nc.vector.tensor_scalar((w.q, w.k, w.vv)[j], y, b_qkv[:, j:j + 1], s_yat[:, j:j + 1],
                                        ALU.add, ALU.mult).then_inc(w.sem("A", "qkv"), 1)
            own(nc.vector.tensor_copy(w.n2, w.bank(0)))
            denominator(0)
            yield
            denominator(1)
            yield
            quotient(0)
            yield
            denominator(2)
            quotient(1)
            yield
            dve.wait_ge(w.sem("A", "qq"), i * 2 + 2)
            nc.vector.tensor_tensor(w.qq, w.qq, w.kk, ALU.add).then_inc(w.sem("A", "s2"), 1)
            quotient(2)
            yield
            dve.wait_ge(w.sem("A", "nn"), i + 1)
            nc.vector.tensor_scalar(w.nv, w.bank(0)[:, 0:NT * H], ATT_EPS, 0.5, ALU.add, ALU.mult)\
              .then_inc(w.sem("A", "nv"), 1)
            yield
            dve.wait_ge(w.sem("A", "c"), i + 1)
            newton(own, w.nv, w.c, w.cs, w.sem("A", "cs"), w.cx)
            yield from split_dve(dve, "A", w, i, 0, w.k, w.pk)
            dve.wait_ge(w.sem("A", "vt"), i + 1)
            values_to_groups(own, w, i, 1)
            yield
            dve.wait_ge(w.sem("A", "cb"), i + 1)
            nc.vector.tensor_tensor(w.q, w.q, w.bank(2), ALU.mult).then_inc(w.sem("A", "qkv"), 1)
            dve.wait_ge(w.sem("A", "qkv"), i * 4 + 4)
            yield
            yield from split_dve(dve, "A", w, i, 1, w.q, w.pq)
            assert own.n == OWN["dveA"]

        def c_dve(dve, w, i):
            own = Order(dve, w.sem("N", "dve"), own_base("dve", "C", i))
            yield from attn_out_dve(dve, own, "C", w, i, i, bo0_sb[:, 0:1], GA)
            yield from norm_dve(dve, own, w, i * 2 + TURNS, SB, CB)
            lg = w.t[:, 0:32].rearrange("p (t e) -> p t e", e=EX)
            l2 = w.t[:, 32:64].rearrange("p (t e) -> p t e", e=EX)
            tiny = w.tiny
            by_expert = lambda v: v[:, :].unsqueeze(1).broadcast_to([P, NT, EX])
            by_token = lambda c: tiny[:, c:c + NT].unsqueeze(2).broadcast_to([P, NT, EX])
            dve.wait_ge(w.sem("C", "lg"), i + 1)
            own(nc.vector.tensor_tensor(lg, w.bank(3)[:, 0:32].rearrange("p (t e) -> p t e", e=EX),
                                        by_expert(gb_sb), ALU.add))
            own(nc.vector.tensor_tensor(l2, lg, lg, ALU.mult))
            own(nc.vector.reduce_sum(tiny[:, 8:12], l2, axis=AX_X))
            nc.vector.tensor_scalar(tiny[:, 0:4], tiny[:, 8:12], 1 / EX, RMS_EPS, ALU.mult, ALU.add)\
              .then_inc(w.sem("C", "ms"), 1)
            yield
            dve.wait_ge(w.sem("C", "rms"), i + 1)
            newton(own, tiny[:, 0:4], tiny[:, 4:8], tiny[:, 16:20], None)
            own(nc.vector.tensor_tensor(lg, lg, by_token(4), ALU.mult))
            own(nc.vector.tensor_tensor(lg, lg, by_expert(rms_sb), ALU.mult))
            own(nc.vector.reduce_max(tiny[:, 8:12], lg, axis=AX_X))
            nc.vector.tensor_tensor(lg, lg, by_token(8), ALU.subtract).then_inc(w.sem("C", "lm"), 1)
            yield
            dve.wait_ge(w.sem("C", "le"), i + 1)
            own(nc.vector.reduce_sum(tiny[:, 16:20], l2, axis=AX_X))
            own(nc.vector.tensor_scalar(tiny[:, 16:20], tiny[:, 16:20], NORM_EPS, 1.0, ALU.mult, ALU.add))
            nc.vector.reciprocal(tiny[:, 12:16], tiny[:, 16:20]).then_inc(w.sem("C", "ng"), 1)
            yield
            dve.wait_ge(w.sem("O", "down"), i * EU + (EU + DOWN0))
            own(nc.vector.tensor_scalar(w.y, w.bank(2), b2s[:, 0:1], None, ALU.add))
            dve.wait_ge(w.sem("C", "ngb"), i + 1)
            own(nc.vector.tensor_tensor(w.y, w.y, w.bank(3), ALU.mult))
            nc.vector.scalar_tensor_tensor(w.xb, w.y, w.mb[:, GB:GB + 1], w.xb, ALU.mult, ALU.add)\
              .then_inc(w.sem("N", "x"), 1)
            yield
            yield from norm_dve(dve, own, w, i * 2 + (TURNS + 1), 6 + SA, 6 + CA)
            dve.wait_ge(w.sem("C", "kvq"), i * 2 + 1)
            nc.vector.tensor_copy(w.kv, w.bank(3)).then_inc(w.sem("C", "copied"), 1)
            yield
            dve.wait_ge(w.sem("C", "lat"), i + 1)
            nc.vector.tensor_copy(w.lat[0:32, :], w.bank(0)[0:32, :]).then_inc(w.sem("C", "copied"), 1)
            yield
            yield from split_dve(dve, "C", w, i, 0, w.bank(2), w.pq)
            dve.wait_ge(w.sem("C", "rec"), i + 1)
            values_to_groups(own, w, i, 3)
            yield
            yield from split_dve(dve, "C", w, i, 1, w.bank(1), w.pk)
            assert own.n == OWN["dveC"]

        def e_dve(dve, w, i):
            own = Order(dve, w.sem("N", "dve"), own_base("dve", "E", i))
            yield from attn_out_dve(dve, own, "E", w, i, i + TURNS, None, 6 + GA)
            yield from norm_dve(dve, own, w, i + 3 * TURNS, 6 + SB, 6 + CB)
            dve.wait_ge(w.sem("E", "rows"), i + 1)
            own(nc.vector.tensor_copy(w.ev, w.bank(2)[0:32, 0:2 * P].rearrange("p (k c) -> p k c", k=2)))
            for m in range(MU):
                ins = nc.vector.tensor_scalar(w.evm[0:32, m * P:(m + 1) * P], w.ev[:, 0, :],
                                              ident[0:32, 2 * m:2 * m + 1], None, ALU.mult)
                if m < MU - 1:
                    own(ins)
                else:
                    ins.then_inc(w.sem("E", "ev"), 1)
            yield
            turned = w.ev[:, 0, :].rearrange("p (r t) -> p t r", t=MU)
            for m in range(MU):
                dst = w.ev2[0:32, :].rearrange("p (t i r) -> p t i r", t=MU, i=MU)[:, :, m, :]
                ins = nc.vector.tensor_scalar(dst, turned, ident[0:32, 2 * MU + 2 * m:2 * MU + 2 * m + 1],
                                              None, ALU.mult)
                if m < MU - 1:
                    own(ins)
                else:
                    ins.then_inc(w.sem("E", "ev"), 1)
            yield
            dve.wait_ge(w.sem("E", "delta"), i * 2 + 1)
            nc.vector.scalar_tensor_tensor(w.w1e, w.bank(3), sc_sb[:, 0:1], mw1_sb[:, :], ALU.mult, ALU.add)\
              .then_inc(w.sem("E", "weights"), 1)
            yield
            dve.wait_ge(w.sem("E", "delta"), i * 2 + 2)
            nc.vector.scalar_tensor_tensor(w.w2e, w.bank(2), sc_sb[:, 0:1],
                                           mw2_sb[:, :, :].rearrange("p u d -> p (u d)"), ALU.mult, ALU.add)\
              .then_inc(w.sem("E", "weights"), 1)
            yield
            dve.wait_ge(w.sem("O", "down"), i * MU + (BEFORE["E"] + MU + DOWN0))
            own(nc.vector.tensor_scalar(w.y, w.bank(2), mb2_sb[:, 0:1], w.mb[:, 6 + GB:7 + GB], ALU.add, ALU.mult))
            dve.wait_ge(w.sem("E", "outd"), i * 16 + 16)
            nc.vector.tensor_tensor(w.res, w.y, w.xb, ALU.add).then_inc(w.sem("E", "res"), 1)
            assert own.n == OWN["dveE"]

        @block.vector
        def _(dve):
            nc.vector.memset(qst[:, :, :, :], 0.0).then_inc(sem("zeros"), 1)
            nc.vector.memset(kst[:, :, :, :], 0.0).then_inc(sem("zeros"), 1)
            dve.wait_ge(sem("loaded"), LOADED)
            own = Order(dve, sem("P_dve"), 0)
            dve.wait_ge(sem("sil_e"), 1)
            own(nc.vector.tensor_scalar(sil[:, 1], sil[:, 0], 1.0, None, ALU.add))
            own(nc.vector.reciprocal(sil[:, 2], sil[:, 1]))
            nc.vector.tensor_tensor(sil[:, 3], c_sb[:, :, :], sil[:, 2], ALU.mult).then_inc(sem("sil"), 1)
            nc.vector.tensor_tensor(work[0].d[0][:, 0:3 * D].rearrange("p (j d) -> p j d", j=3), w_qkv[:, :, :],
                                    w_qkv[:, :, :], ALU.mult).then_inc(sem("wsq"), 1)
            dve.wait_ge(sem("wsq"), 1)
            own(nc.vector.tensor_scalar(w_qkv[:, :, :], w_qkv[:, :, :], -2.0, None, ALU.mult))
            dve.wait_ge(sem("modps"), 1)
            own(nc.vector.tensor_copy(mod[:, :, :].rearrange("p b m -> p m b"),
                                      ps[:, 0, 0:12 * B].rearrange("p (m b) -> p m b", b=B)))
            gains, g = (mod[:, :, m::CB - CA] for m in (CA, GA))
            own(nc.vector.tensor_scalar(gains, gains, 1.0, None, ALU.add))
            size, sign = (tinies[:, 0, n * 4 * B:(n + 1) * 4 * B].rearrange("p (b m) -> p b m", b=B) for n in range(2))
            own(nc.vector.tensor_scalar(size, g, -1.0, 0.25, ALU.mult, ALU.max))
            own(nc.vector.tensor_tensor(size, size, g, ALU.max))
            own(nc.vector.tensor_scalar(sign, g, 0.0, 2.0, ALU.is_ge, ALU.mult))
            own(nc.vector.tensor_scalar(sign, sign, -1.0, None, ALU.add))
            own(nc.vector.tensor_tensor(g, size, sign, ALU.mult))
            nc.vector.reduce_sum(b2s[:, :], b2_sb[:, :], axis=AX_X).then_inc(sem("mod"), 1)
            dve.wait_ge(sem("wn"), 1)
            nc.vector.tensor_scalar(wn[:, :], ps[:, 4, 0:3], ATT_EPS, None, ALU.add).then_inc(sem("wns"), 1)
            dve.wait_ge(sem("mod"), 1)
            dve.wait_ge(sem("wns"), 1)
            dve.wait_ge(sem("yat"), 1)

            with dve.Fori(0, TURNS) as i:
                in_turns(*(a_dve(dve, w, i) for w in work))
            dve.wait_ge(sem("loaded"), ALL_LOADED)
            attn1_dve(dve)
            with dve.Fori(0, TURNS) as i:
                in_turns(*(c_dve(dve, w, i) for w in work))
            attn2_dve(dve)
            with dve.Fori(0, TURNS) as i:
                in_turns(*(e_dve(dve, w, i) for w in work))


def kernel(**inputs):
    import concourse.bacc as bacc
    from concourse.bass_utils import run_bass_kernel_spmd

    a = {k: np.asarray(v) for k, v in inputs.items()}
    col = lambda v: np.ascontiguousarray(v.reshape(-1, 1))
    d = np.arange(D)
    i = np.arange(S, dtype=np.float32)
    decay = np.exp(-np.float32(0.01) * np.abs(i[:, None] - i[None, :])).astype(np.float32)
    consts = np.stack([np.full((D, D), 1 / D), d[:, None] // DH == d[None, :] // DH, np.ones((D, D))],
                      axis=1).astype(np.float32)
    lay = {
        "xT": a["L0_attn_inputs_q"].reshape(B * S, D).T,
        "cT": np.stack([a["L0_c"].T, a["L1_c"].T], axis=1),
        "wmod": np.stack([a["L0_wmod"], a["L1_wmod"]], axis=1),
        "wqkv": np.stack([a["L0_attn_wq"], a["L0_attn_wk"], a["L0_attn_wv"]], axis=1),
        "bqkv": np.stack([a["L0_attn_bq"], a["L0_attn_bk"], a["L0_attn_bv"]], axis=1),
        "alpha": np.concatenate([a["L0_attn_aq"], a["L0_attn_ak"], a["L0_attn_av"]]),
        "wo0": a["L0_attn_wo"], "bo0": col(a["L0_attn_bo"]),
        "gwT": a["L0_ffn_gate_w"].T, "gb": a["L0_ffn_gate_b"], "rms": a["L0_ffn_rms_w"],
        "w1": a["L0_ffn_w1"].transpose(1, 0, 2).reshape(D, EU, P),
        "b1": a["L0_ffn_b1"].reshape(EU, P).T,
        "w2": a["L0_ffn_w2"].reshape(EU, P, D).transpose(1, 0, 2),
        "b2": a["L0_ffn_b2"].T,
        "l1w": np.stack([a["L1_attn_W_q"], a["L1_attn_W_k"], a["L1_attn_W_v"]], axis=1),
        "l1down": a["L1_attn_W_down_kv"],
        "l1up": np.stack([a["L1_attn_W_up_k"], a["L1_attn_W_up_v"]], axis=1),
        "l1wo": a["L1_attn_W_o"],
        "mw1": a["L1_ffn_W1"].T, "mb1": a["L1_ffn_b1"].reshape(MU, P).T,
        "mw2": a["L1_ffn_W2"].T.reshape(MU, P, D).transpose(1, 0, 2), "mb2": col(a["L1_ffn_b2"]),
        "scale": a["L1_ffn_scale"].reshape(1),
        "ident_in": np.eye(P, dtype=np.float32),
        "blk_in": consts,
        "decay_in": decay.reshape(NT, P, S).transpose(1, 0, 2),
    }
    nc = bacc.Bacc("TRN2", target_bir_lowering=False, num_devices=1)
    arrays, args = {}, {}
    for name, v in lay.items():
        arrays[f"in_{name}"] = np.ascontiguousarray(v)
        args[name] = nc.dram_tensor(f"in_{name}", v.shape, mybir.dt.from_np(v.dtype), kind="ExternalInput").ap()
    x1 = nc.dram_tensor("x1", (D, B * S), F32, kind="Internal").ap()
    parts = nc.dram_tensor("parts", (2, 2, B, H, SPLITS, DH, S), BF16, kind="Internal").ap()
    out = nc.dram_tensor("out_0", (D, B * S), F32, kind="ExternalOutput").ap()
    build(nc, parts=parts, x1=x1, out=out, **args)
    r = run_bass_kernel_spmd(nc, [arrays], core_ids=[0])
    return np.ascontiguousarray(r.results[0]["out_0"].T).reshape(B, S, D)
```
